# Optimizing a Trainium2 kernel written in Bass

```python
import numpy as np
import jax
import jax.numpy as jnp

def _softmax(x, axis=-1):
    return jax.nn.softmax(x, axis=axis)

def _gelu(x):
    return jax.nn.gelu(x, approximate=True)

def _silu(x):
    return jax.nn.silu(x)

def _sigmoid(x):
    return jax.nn.sigmoid(x)

def _layernorm(x, axis=-1, eps=1e-05):
    m = jnp.mean(x, axis=axis, keepdims=True)
    v = jnp.var(x, axis=axis, keepdims=True)
    return (x - m) / jnp.sqrt(v + eps)

def _scatter_add(tgt, idx, src, axis=0):
    return tgt.at[idx].add(src)

def _segment_sum(src, seg, n):
    return jax.ops.segment_sum(src, seg, n)
kernel_name = 'mk_seq_postln_d1_jaxref_r8_536120'

def setup_inputs(seed: int=0):
    np.random.seed(seed)
    _w = jnp.asarray

    def _L0_attn_setup():
        import jax, jax.numpy as jnp
        import numpy as np
        D_HEAD = 128
        ROTARY_BASE = 1250
        INF_APPROX = 1e+30

        def _rope(x):
            B, T, H, D = x.shape
            pos = jnp.arange(T, dtype=jnp.float32)
            dims = jnp.arange(D // 2, dtype=jnp.float32)
            ang_freqs = jnp.power(float(ROTARY_BASE), -dims / (D // 2))
            radians = pos[:, None] * ang_freqs[None, :]
            cos = jnp.cos(radians)[None, :, None, :].astype(x.dtype)
            sin = jnp.sin(radians)[None, :, None, :].astype(x.dtype)
            even, odd = jnp.split(x, 2, axis=-1)
            return jnp.concatenate([even * cos - odd * sin, even * sin + odd * cos], axis=-1)
        key = jax.random.key(seed)
        kx, kq, kk, kv, ko = jax.random.split(key, 5)
        B, T, M, H, D = (2, 256, 256, 16, 128)
        n_layer = 24
        x = jax.random.normal(kx, (B, T, M), dtype=jnp.float32)
        w_aq = jax.random.normal(kq, (H, M, D), dtype=jnp.float32) * M ** (-0.5)
        w_ak = jax.random.normal(kk, (H, M, D), dtype=jnp.float32) * M ** (-0.5)
        w_av = jax.random.normal(kv, (H, M, D), dtype=jnp.float32) * M ** (-0.5)
        w_ao = jax.random.normal(ko, (H, D, M), dtype=jnp.float32) * (2 * M * n_layer) ** (-0.5)
        return {'x': x, 'w_aq': w_aq, 'w_ak': w_ak, 'w_av': w_av, 'w_ao': w_ao}
    _L0_attn_in = _L0_attn_setup()

    def _L0_ffn_setup():
        import jax, jax.numpy as jnp
        import numpy as np
        DIM = 256
        EXPERT_DIM = 128
        N_EXPERTS = 16
        TOPK = 2
        N_SHARED = 1
        B, T = (4, 256)
        key = jax.random.key(seed)
        ks = jax.random.split(key, 9)
        s = 0.02
        return {'x': jax.random.normal(ks[0], (B, T, DIM), jnp.float32), 'router_w': jax.random.normal(ks[1], (N_EXPERTS, DIM), jnp.float32) * s, 'router_bias': jnp.zeros((N_EXPERTS,), jnp.float32), 'Wu': jax.random.normal(ks[2], (N_EXPERTS, DIM, EXPERT_DIM), jnp.float32) * s, 'Wg': jax.random.normal(ks[3], (N_EXPERTS, DIM, EXPERT_DIM), jnp.float32) * s, 'Wd': jax.random.normal(ks[4], (N_EXPERTS, EXPERT_DIM, DIM), jnp.float32) * s, 'Su': jax.random.normal(ks[5], (N_SHARED, DIM, EXPERT_DIM * TOPK), jnp.float32) * s, 'Sg': jax.random.normal(ks[6], (N_SHARED, DIM, EXPERT_DIM * TOPK), jnp.float32) * s, 'Sd': jax.random.normal(ks[7], (N_SHARED, EXPERT_DIM * TOPK, DIM), jnp.float32) * s}
    _L0_ffn_in = _L0_ffn_setup()
    _d = {'L0_attn_x': _L0_attn_in['x'], 'L0_attn_w_aq': _L0_attn_in['w_aq'], 'L0_attn_w_ak': _L0_attn_in['w_ak'], 'L0_attn_w_av': _L0_attn_in['w_av'], 'L0_attn_w_ao': _L0_attn_in['w_ao'], 'L0_ffn_router_w': _L0_ffn_in['router_w'], 'L0_ffn_router_bias': _L0_ffn_in['router_bias'], 'L0_ffn_Wu': _L0_ffn_in['Wu'], 'L0_ffn_Wg': _L0_ffn_in['Wg'], 'L0_ffn_Wd': _L0_ffn_in['Wd'], 'L0_ffn_Su': _L0_ffn_in['Su'], 'L0_ffn_Sg': _L0_ffn_in['Sg'], 'L0_ffn_Sd': _L0_ffn_in['Sd']}
    _x0 = _d['L0_attn_x']
    _d['L0_attn_x'] = jax.random.normal(jax.random.fold_in(jax.random.key(seed), 1), (1, 1024, 256), dtype=_x0.dtype)
    del _x0
    return _d

def reference(L0_attn_x, L0_attn_w_aq, L0_attn_w_ak, L0_attn_w_av, L0_attn_w_ao, L0_ffn_router_w, L0_ffn_router_bias, L0_ffn_Wu, L0_ffn_Wg, L0_ffn_Wd, L0_ffn_Su, L0_ffn_Sg, L0_ffn_Sd):

    def _L0_attn_ref(x, w_aq, w_ak, w_av, w_ao):
        import jax, jax.numpy as jnp
        import numpy as np
        D_HEAD = 128
        ROTARY_BASE = 1250
        INF_APPROX = 1e+30

        def _rope(x):
            B, T, H, D = x.shape
            pos = jnp.arange(T, dtype=jnp.float32)
            dims = jnp.arange(D // 2, dtype=jnp.float32)
            ang_freqs = jnp.power(float(ROTARY_BASE), -dims / (D // 2))
            radians = pos[:, None] * ang_freqs[None, :]
            cos = jnp.cos(radians)[None, :, None, :].astype(x.dtype)
            sin = jnp.sin(radians)[None, :, None, :].astype(x.dtype)
            even, odd = jnp.split(x, 2, axis=-1)
            return jnp.concatenate([even * cos - odd * sin, even * sin + odd * cos], axis=-1)
        q = jnp.einsum('btm,hmd->bthd', x, w_aq)
        k = jnp.einsum('btm,hmd->bthd', x, w_ak)
        v = jnp.einsum('btm,hmd->bthd', x, w_av)
        q = _rope(q)
        k = _rope(k)
        s = jnp.einsum('bihd,bjhd->bhij', q, k) / D_HEAD
        T = x.shape[1]
        i = jnp.arange(T)[:, None]
        j = jnp.arange(T)[None, :]
        mask = (i < j).astype(s.dtype)[None, None, :, :]
        s = s - INF_APPROX * mask
        p = jax.nn.softmax(s, axis=-1)
        o = jnp.einsum('bhij,bjhd->bihd', p, v)
        r = jnp.einsum('bihd,hdm->bim', o, w_ao)
        return r

    def _L0_ffn_ref(x, router_w, router_bias, Wu, Wg, Wd, Su, Sg, Sd):
        import jax, jax.numpy as jnp
        import numpy as np
        DIM = 256
        EXPERT_DIM = 128
        N_EXPERTS = 16
        TOPK = 2
        N_SHARED = 1
        B, T = (4, 256)
        Bx, Tx, D = x.shape
        flat = x.reshape(Bx * Tx, D)
        logits = flat @ router_w.T
        scores = jax.nn.softmax(logits, axis=-1)
        _, topk_idx = jax.lax.top_k(logits + router_bias, TOPK)
        topk_scores = jnp.take_along_axis(scores, topk_idx, axis=-1)
        topk_scores = topk_scores / topk_scores.sum(-1, keepdims=True)
        combine = jnp.einsum('nk,nke->ne', topk_scores, jax.nn.one_hot(topk_idx, N_EXPERTS, dtype=scores.dtype))
        out = jnp.zeros_like(flat)
        for e in range(N_EXPERTS):
            h = jax.nn.silu(flat @ Wu[e]) * (flat @ Wg[e])
            out = out + combine[:, e:e + 1] * (h @ Wd[e])
        for s in range(N_SHARED):
            out = out + jax.nn.silu(flat @ Su[s]) * (flat @ Sg[s]) @ Sd[s]
        return out.reshape(Bx, Tx, D)
    x = L0_attn_x
    x = _layernorm(x + _L0_attn_ref(x, L0_attn_w_aq, L0_attn_w_ak, L0_attn_w_av, L0_attn_w_ao), axis=-1)
    x = _layernorm(x + _L0_ffn_ref(x, L0_ffn_router_w, L0_ffn_router_bias, L0_ffn_Wu, L0_ffn_Wg, L0_ffn_Wd, L0_ffn_Su, L0_ffn_Sg, L0_ffn_Sd), axis=-1)
    return x

_drawn_inputs = setup_inputs


def setup_inputs(seed=0):
    import zlib

    import numpy as np

    out = dict(_drawn_inputs(seed))
    spreads = {'L0_ffn_router_bias': (0.0, 0.8)}
    factors = {'L0_attn_w_aq': 8.0,
     'L0_attn_w_ak': 8.0,
     'L0_ffn_router_w': 7.161,
     'L0_ffn_Wu': 6.7,
     'L0_ffn_Wg': 6.616,
     'L0_ffn_Wd': 6.584,
     'L0_ffn_Su': 3.395,
     'L0_ffn_Sg': 3.353,
     'L0_ffn_Sd': 3.352}
    for name, (base, spread) in spreads.items():
        noise = np.random.default_rng([zlib.crc32(name.encode()), seed]).standard_normal(out[name].shape)
        drawn = base * np.exp(spread * noise) if base else spread * noise
        out[name] = jnp.asarray(drawn.astype(out[name].dtype))
    for name, factor in factors.items():
        out[name] = (out[name] * factor).astype(out[name].dtype)
    return out
```

```python
from contextlib import ExitStack

import numpy as np

import concourse.bass as bass
from concourse import mybir

F32 = mybir.dt.float32
F32R = mybir.dt.float32r
BF16 = mybir.dt.bfloat16
U32 = mybir.dt.uint32
ALU = mybir.AluOpType
ACT = mybir.ActivationFunctionType
AX = mybir.AxisListType

P = 128
T, M = 1024, 256
H, D = 16, 128
E, F = 16, 128
NS = 2
MC = M // P
NT = T // P
W = 512
NW = T // W
GT = W // P
EPS = 1e-5
MASKED = -1e30
ROTARY_BASE = 1250

TURNS = {0: [(0, 0, 0), (1, 1, 1)], 1: [(2, 2, 0)], 2: [(4, 3, 0)], 3: [(5, 4, 0)], 4: [(6, 5, 0)],
         5: [(7, 6, 0), (8, 7, 1)], 6: [(10, 8, 0), (11, 9, 1)], 7: [(12, 10, 0), (13, 11, 1)]}
SPREAD = {1: 3, 5: 9}
NEVENT, NTURN = 14, 12


def need(eng, sem, count):
    if not isinstance(count, int) or count > 0:
        eng.wait_ge(sem, count)


def event_no(f, k):
    if isinstance(f, int) and f <= 0:
        return 0 if f < 0 or k in (0, 1, 3) else (1 if k == 2 else k - 2)
    if isinstance(f, int) and f == H and k == SPREAD[1]:
        k -= 1
    return NEVENT * f + k - 2


def turn_no(f, j):
    return NTURN * f + j - 1


def three(eng, out, a, b, start, stop):
    eng.matmul(out, a[0], b[0], start=start, stop=False)
    eng.matmul(out, a[0], b[1], start=False, stop=False)
    return eng.matmul(out, a[1], b[0], start=False, stop=stop)


def turned_at(f, i):
    return (f, i) not in ((0, 0), (H, 1))


def attend_walk(eng, step):
    for i in range(NT):
        step(0, 0, 0, i)
    with eng.Fori(0, 3) as it:
        for s in range(NT, 5 * NT):
            step(4 * it + s // NT, 2 * it + s // NT // 2, s // NT, s % NT)
    for s in range(13 * NT, H * NT):
        step(s // NT, s // NT // 2, s // NT, s % NT)
    step(H, H // 2, H, 0)
    step(H, H // 2, H, 1)


def chunk_at(f, p, fs, i):
    first, last = isinstance(f, int) and f == 0, isinstance(f, int) and f == H - 1
    if last or isinstance(f, int) and f == H:
        return None
    if fs % 2 == 0:
        kind = ["q0", "k0", "o00", "o10", "q1", "k1", "o01", "o11"][i]
        if kind[0] == "o" and first:
            return None
        number = 8 + [1, 2, 0, 0, 3, 4, 0, 0][i] if first else 8 * f + 5 + i
        return kind, number, 12 * p + 8 + [1, 2, 2, 2, 3, 4, 4, 4][i]
    return ["q0", "k0", "q1", "k1", "v0", "v1", "v2", "v3"][i], 8 * f + 5 + i, 12 * p + 13 + i


def attention(nc, ctx, x, wq, wk, wv, wo, cos_t, sin_t, r_acc):
    def sb(name, shape, dt=F32):
        return ctx.enter_context(nc.sbuf_tensor(name, shape, dt))

    def sem(name):
        return ctx.enter_context(nc.semaphore(name))

    xT = [sb("xT_hi", [P, MC, T], F32R), sb("xT_lo", [P, MC, T], F32R)]
    cos = sb("cos", [P, T])
    sin = sb("sin", [P, T])
    ident = sb("ident_a", [P, P])
    ident_b = sb("ident_b", [P, P], BF16)
    mask = sb("mask", [P, P], BF16)
    raw_qk = [sb(f"raw_qk{s}", [P, 2, MC, D]) for s in range(2)]
    raw_v = sb("raw_v", [P, MC, 2, D])
    raw_o = sb("raw_o", [P, 2, M])
    w_qk = [[sb(f"w_qk{n}{s}", [P, 2, MC, D], F32R) for s in range(2)] for n in range(2)]
    w_v = [sb(f"w_v{n}", [P, MC, 2, D], F32R) for n in range(2)]
    w_o = [sb(f"w_o{n}", [P, 2, M], F32R) for n in range(2)]
    swapped = [sb(f"swapped{s}", [P, W]) for s in range(2)]
    rotated = [sb(f"rotated{s}", [P, W]) for s in range(2)]
    QT = [[sb(f"QT{n}{s}", [P, T], F32R) for s in range(2)] for n in range(2)]
    KT = [[sb(f"KT{n}{s}", [P, T], F32R) for s in range(2)] for n in range(2)]
    V = [[sb(f"V{n}{s}", [P, NT, 2 * D], F32R) for s in range(2)] for n in range(2)]
    probs = sb("probs", [P, 2, T])
    PT = [[sb(f"PT{n}{g}", [P, GT * (g + 1), W], F32R) for g in range(2)] for n in range(2)]
    spread = sb("spread", [P, W])
    o_buf = sb("o_buf", [P, W])
    OT = [[sb(f"OT{n}{s}", [P, T], F32R) for s in range(2)] for n in range(2)]
    neg_max = sb("neg_max", [P, NT])
    row_sum = sb("row_sum", [P, NT])
    recip = sb("recip", [P, NT])
    x_tok = probs[:].rearrange("p s (t m) -> p (s t) m", m=M)

    S_ps = [ctx.enter_context(nc.psum_tensor(f"S{s}", [P, T], F32)) for s in range(2)]
    turn_ps = [ctx.enter_context(nc.psum_tensor(f"turn{s}", [P, W], F32)) for s in range(2)]
    O_ps = ctx.enter_context(nc.psum_tensor("O", [P, W], F32))
    C_ps = ctx.enter_context(nc.psum_tensor("C", [P, W], F32))

    x_in = [sem(f"x_in{t}") for t in range(NT)]
    tables_in = sem("tables_in")
    qk_in = [sem("qk_in0"), sem("qk_in1")]
    v_in, o_in = sem("v_in"), sem("o_in")
    zeroed, consts = sem("zeroed"), sem("consts")
    xT_full, xT_hi, xT_lo = sem("xT_full"), sem("xT_hi"), sem("xT_lo")
    qk_split, v_split, o_split = sem("qk_split"), sem("v_split"), sem("o_split")
    scores_full = sem("scores_full")
    chunk_full = sem("chunk_full")
    turn_full = sem("turn_full")
    values_full = sem("values_full")
    max_ready = sem("max_ready")
    probs_ready = sem("probs_ready")
    turn_hi = sem("turn_hi")
    turn_lo = sem("turn_lo")
    chunk_act = sem("chunk_act")
    chunk_dve = sem("chunk_dve")
    recip_ready = sem("recip_ready")
    o_scaled = sem("o_scaled")
    o_parted = sem("o_parted")
    roped = sem("roped")
    pool_step = sem("pool_step")
    waited = sem("waited")

    block = ctx.enter_context(nc.Block())

    @block.sync
    def _(sp):
        sp.dma_start(raw_qk[0][:, 0], wq[0].rearrange("(c p) d -> p c d", p=P)).then_inc(qk_in[0], 16)
        sp.dma_start(raw_qk[0][:, 1], wk[0].rearrange("(c p) d -> p c d", p=P)).then_inc(qk_in[0], 16)
        for t in range(NT):
            sp.dma_start(x_tok[:, t], x[0, t * P:(t + 1) * P, :]).then_inc(x_in[t], 16)
        sp.dma_start(cos[:], cos_t).then_inc(tables_in, 16)
        sp.dma_start(sin[:], sin_t).then_inc(tables_in, 16)

        def load_qk(h, slot):
            for n, w in ((0, wq), (1, wk)):
                sp.dma_start(raw_qk[slot][:, n], w[bass.ds(h, 1)].rearrange("o (c p) d -> p (o c) d", p=P)
                             ).then_inc(qk_in[slot], 16)

        def load_v(pair):
            for n in range(2):
                sp.dma_start(raw_v[:, :, n], wv[bass.ds(2 * pair + n, 1)].rearrange(
                    "o (c p) d -> p (o c) d", p=P)).then_inc(v_in, 16)

        def load_o(pair):
            sp.dma_start(raw_o[:], wo[bass.ds(2 * pair, 2)].rearrange("n d m -> d n m")).then_inc(o_in, 16)

        load_v(0)
        load_qk(1, 1)
        load_o(0)
        sp.wait_ge(qk_split, 1)
        load_qk(2, 0)
        sp.wait_ge(v_split, 1)
        load_v(1)

        def frame(f, p, fs):
            last = f if isinstance(f, int) else 0
            if last + 3 < H:
                sp.wait_ge(qk_split, f + 2)
                load_qk(f + 3, (fs + 3) % 2)
            if fs % 2 == 1:
                if last // 2 + 2 < H // 2:
                    sp.wait_ge(v_split, p + 2)
                    load_v(p + 2)
                if last // 2 + 1 < H // 2:
                    sp.wait_ge(o_split, p + 1)
                    load_o(p + 1)

        frame(0, 0, 0)
        with sp.Fori(0, 3) as it:
            for fs in range(1, 5):
                frame(4 * it + fs, 2 * it + fs // 2, fs)
        for f in range(13, H):
            frame(f, f // 2, f)

    @block.gpsimd
    def _(pool):
        nc.gpsimd.memset(ident[:], 0.0).then_inc(zeroed, 1)
        nc.gpsimd.memset(ident_b[:], 0.0).then_inc(zeroed, 1)
        nc.gpsimd.memset(mask[:], 0.0).then_inc(zeroed, 1)
        nc.gpsimd.memset(r_acc[:], 0.0).then_inc(zeroed, 1)
        pool.wait_ge(zeroed, 4)
        for m in (ident, ident_b):
            nc.gpsimd.affine_select(out=m[:], in_=m[:], compare_op=ALU.not_equal, fill=1.0, base=0,
                                    pattern=[[-1, P]], channel_multiplier=1).then_inc(consts, 1)
        nc.gpsimd.affine_select(out=mask[:], in_=mask[:], compare_op=ALU.is_ge, fill=MASKED, base=0,
                                pattern=[[-1, P]], channel_multiplier=1).then_inc(consts, 1)
        done = [0, 0]

        def part(raw, hi, lo, ready):
            pool.sem_inc(waited, 1)
            nc.gpsimd.tensor_copy(hi, raw).then_inc(pool_step, 1)
            done[1] += 1
            pool.wait_ge(pool_step, done[0] + done[1])
            nc.gpsimd.tensor_tensor(lo, raw, hi.bitcast(F32), ALU.subtract).then_inc(ready, 1)

        def part_qk(h, half, slot):
            pool.wait_ge(qk_in[slot], 32 * (half + 1))
            part(raw_qk[slot][:], w_qk[0][slot][:], w_qk[1][slot][:], qk_split)

        def part_v(pair):
            pool.wait_ge(v_in, 32 * (pair + 1))
            part(raw_v[:], w_v[0][:], w_v[1][:], v_split)

        def part_o(pair):
            pool.wait_ge(o_in, 16 * (pair + 1))
            part(raw_o[:], w_o[0][:], w_o[1][:], o_split)

        def rope(kind, dst, number, act_no, dve_no):
            slot, half = "qk".index(kind[0]), int(kind[1])
            cols = slice(half * W, (half + 1) * W)
            pool.wait_ge(chunk_act, act_no)
            nc.gpsimd.tensor_tensor(swapped[slot][:], swapped[slot][:], sin[:, cols], ALU.mult
                                    ).then_inc(pool_step, 1)
            done[1] += 1
            pool.wait_ge(pool_step, done[0] + done[1])
            pool.wait_ge(chunk_dve, dve_no)
            nc.gpsimd.tensor_tensor(rotated[slot][:], rotated[slot][:], swapped[slot][:], ALU.add
                                    ).then_inc(pool_step, 1)
            done[1] += 1
            pool.wait_ge(pool_step, done[0] + done[1])
            bufs = QT if kind[0] == "q" else KT
            part(rotated[slot][:], bufs[0][dst][:, cols], bufs[1][dst][:, cols], roped)

        def part_out(f, fs, g):
            cols = slice(g * W, (g + 1) * W)
            pool.wait_ge(o_scaled, 2 * f + g + 1)
            part(o_buf[:], OT[0][fs % 2][:, cols], OT[1][fs % 2][:, cols], o_parted)

        def step(f, p, fs, i):
            at = f if isinstance(f, int) else 1
            ch = chunk_at(f, p, fs, i)
            if ch and ch[0][0] in "qk":
                rope(ch[0], (fs + 1) % 2, None, ch[2], ch[1])
            if i == 1 and at > 0:
                part_out(f - 1, fs - 1, 1)
            if i == 5 and at < H:
                part_out(f, fs, 0)
            if i == 3 and fs % 2 == 0 and at // 2 + 1 < H // 2:
                pool.wait_ge(chunk_full, 8 if at == 0 else 16 * p + 4)
                part_v(p + 1)
            if i == 4 and fs % 2 == 1:
                pool.wait_ge(chunk_full, 16 * p + 12)
                part_o(p)
            if i == 7 and at + 2 < H:
                part_qk(f + 2, p + 1, fs % 2)

        part_qk(0, 0, 0)
        part_v(0)
        pool.wait_ge(tables_in, 32)
        for n, kind in enumerate(["q0", "k0", "q1", "k1"]):
            rope(kind, 0, None, n + 1, n + 1)
        part_qk(1, 0, 1)
        for i in range(NT):
            step(0, 0, 0, i)
        before = done[1]
        with pool.Fori(0, 3) as it:
            loop_steps = 4 * (4 * 3 + 2 + 1) + 2 + 2
            done[0] = loop_steps * it
            for s in range(NT, 5 * NT):
                step(4 * it + s // NT, 2 * it + s // NT // 2, s // NT, s % NT)
        assert done[1] - before == loop_steps, done[1] - before
        done[0] = 2 * loop_steps
        for s in range(13 * NT, H * NT):
            step(s // NT, s // NT // 2, s // NT, s % NT)
        step(H, H // 2, H, 0)
        step(H, H // 2, H, 1)

    @block.scalar
    def _(act):
        for n in range(NW * MC):
            c, w = n // NW, n % NW
            act.wait_ge(xT_full, n + 1)
            nc.scalar.activation(xT[0][:, c, w * W:(w + 1) * W], S_ps[c][:, w * W:(w + 1) * W],
                                 ACT.Copy).then_inc(xT_hi, 1)

        def read_chunk(kind, pair_slot, number, act_no, rope_no):
            act.wait_ge(chunk_full, number)
            if kind[0] in "qk":
                slot, scale = "qk".index(kind[0]), (1.0 / D if kind[0] == "q" else 1.0)
                need(act, roped, rope_no - 2)
                nc.scalar.activation(swapped[slot][0:D // 2], C_ps[D // 2:D, :], ACT.Copy, scale=scale)
                nc.scalar.activation(swapped[slot][D // 2:D], C_ps[0:D // 2, :], ACT.Copy, scale=scale
                                     ).then_inc(chunk_act, 1)
            else:
                t = 2 * int(kind[1])
                nc.scalar.activation(V[0][pair_slot][:, t:t + 2].rearrange("p a b -> p (a b)"), C_ps[:],
                                     ACT.Copy).then_inc(chunk_act, 1)

        def step(f, p, fs, i):
            at = f if isinstance(f, int) else 1
            ch = chunk_at(f, p, fs, i)
            if ch and ch[0][0] != "o":
                read_chunk(ch[0], (fs // 2 + 1) % 2, ch[1], ch[2],
                           4 * f + 5 + ["q0", "k0", "q1", "k1"].index(ch[0]) if ch[0][0] in "qk" else 0)
            if turned_at(at, i):
                tile = i - 1 if i else NT - 1
                for k, _, part in TURNS[i]:
                    act.wait_ge(turn_full, event_no(f, k))
                    g, n = tile // GT, min(GT, tile + 1 - GT * part)
                    nc.scalar.activation(PT[0][g][:, GT * part:GT * part + n, (tile % GT) * P:(tile % GT + 1) * P],
                                         turn_ps[k % 2][:, 0:n * P].rearrange("p (a b) -> p a b", a=n),
                                         ACT.Copy).then_inc(turn_hi, 1)
            if i == 5 and at < H or i == 1 and at > 0:
                k = SPREAD[i]
                act.wait_ge(turn_full, event_no(f, k))
                need(act, o_scaled, 2 * f + (0 if i == 5 else -1))
                nc.scalar.activation(spread[:], turn_ps[k % 2][:], ACT.Copy).then_inc(turn_hi, 1)
            if at < H:
                act.wait_ge(max_ready, NT * f + i + 1)
                w = (i + 1) * P
                nc.scalar.activation(probs[:, i % 2, 0:w], S_ps[i % 2][:, 0:w], ACT.Exp,
                                     bias=neg_max[:, i:i + 1], accum_out=row_sum[:, i:i + 1]
                                     ).then_inc(probs_ready, 1)

        for n, kind in enumerate(["q0", "k0", "q1", "k1", "v0", "v1", "v2", "v3"]):
            read_chunk(kind, 0, n + 1, n + 1, n + 1)
        attend_walk(act, step)

    @block.vector
    def _(dve):
        for n in range(NW * MC):
            c, w = n // NW, n % NW
            dve.wait_ge(xT_hi, n + 1)
            nc.vector.tensor_tensor(xT[1][:, c, w * W:(w + 1) * W], S_ps[c][:, w * W:(w + 1) * W],
                                    xT[0][:, c, w * W:(w + 1) * W].bitcast(F32), ALU.subtract
                                    ).then_inc(xT_lo, 1)

        def read_chunk(kind, pair_slot, number, act_no, rope_no):
            if kind[0] in "qk":
                slot, half = "qk".index(kind[0]), int(kind[1])
                dve.wait_ge(chunk_act, act_no)
                need(dve, roped, rope_no - 2)
                nc.vector.scalar_tensor_tensor(out=rotated[slot][:], in0=C_ps[:],
                                               scalar=1.0 / D if kind[0] == "q" else 1.0,
                                               in1=cos[:, half * W:(half + 1) * W], op0=ALU.mult,
                                               op1=ALU.mult).then_inc(chunk_dve, 1)
            elif kind[0] == "v":
                t = 2 * int(kind[1])
                dve.wait_ge(chunk_act, act_no)
                nc.vector.tensor_tensor(V[1][pair_slot][:, t:t + 2].rearrange("p a b -> p (a b)"), C_ps[:],
                                        V[0][pair_slot][:, t:t + 2].rearrange("p a b -> p (a b)").bitcast(F32),
                                        ALU.subtract).then_inc(chunk_dve, 1)
            else:
                c, w = int(kind[1]), int(kind[2])
                dve.wait_ge(chunk_full, number)
                nc.vector.tensor_tensor(r_acc[:, c, w * W:(w + 1) * W], C_ps[:],
                                        r_acc[:, c, w * W:(w + 1) * W], ALU.add).then_inc(chunk_dve, 1)

        def reciprocals(f, g):
            dve.wait_ge(probs_ready, NT * f + GT * (g + 1))
            nc.vector.reciprocal(recip[:, g * GT:(g + 1) * GT], row_sum[:, g * GT:(g + 1) * GT]
                                 ).then_inc(recip_ready, 1)

        def step(f, p, fs, i):
            at = f if isinstance(f, int) else 1
            if at < H:
                dve.wait_ge(scores_full, NT * f + i + 1)
                nc.vector.tensor_reduce(neg_max[:, i:i + 1], S_ps[i % 2][:, 0:(i + 1) * P], AX.X, ALU.max,
                                        negate=True).then_inc(max_ready, 1)
            ch = chunk_at(f, p, fs, i)
            if ch:
                read_chunk(ch[0], (fs // 2 + 1) % 2, ch[1], ch[2],
                           4 * f + 5 + ["q0", "k0", "q1", "k1"].index(ch[0]) if ch[0][0] in "qk" else 0)
            if turned_at(at, i):
                tile = i - 1 if i else NT - 1
                for k, j, part in TURNS[i]:
                    dve.wait_ge(turn_hi, event_no(f, k))
                    g, n = tile // GT, min(GT, tile + 1 - GT * part)
                    at_ = (slice(None), slice(GT * part, GT * part + n), slice((tile % GT) * P, (tile % GT + 1) * P))
                    nc.vector.tensor_tensor(PT[1][g][at_],
                                            turn_ps[k % 2][:, 0:n * P].rearrange("p (a b) -> p a b", a=n),
                                            PT[0][g][at_].bitcast(F32), ALU.subtract).then_inc(turn_lo, 1)
            if i == 0 and at > 0:
                reciprocals(f - 1, 1)
            if i == 4 and at < H:
                reciprocals(f, 0)
            if i == 5 and at < H or i == 1 and at > 0:
                n = 2 * f + (1 if i == 5 else 0)
                dve.wait_ge(values_full, n)
                dve.wait_ge(turn_hi, event_no(f, SPREAD[i]))
                need(dve, o_parted, n - 1)
                nc.vector.tensor_tensor(o_buf[:], O_ps[:], spread[:], ALU.mult).then_inc(o_scaled, 1)

        dve.wait_ge(tables_in, 32)
        dve.wait_ge(zeroed, 4)
        for n, kind in enumerate(["q0", "k0", "q1", "k1", "v0", "v1", "v2", "v3"]):
            read_chunk(kind, 0, n + 1, n + 1, n + 1)
        attend_walk(dve, step)
        for n in range(4):
            read_chunk(["o00", "o10", "o01", "o11"][n], 0, 8 * (H - 1) + 5 + n, 0, 0)

    @block.tensor
    def _(pe):
        pe.wait_ge(consts, 3)
        for c in range(MC):
            for w in range(NW):
                for q in range(GT):
                    t = w * GT + q
                    pe.wait_ge(x_in[t], 16)
                    ins = pe.transpose(S_ps[c][:, t * P:(t + 1) * P], x_tok[:, t, c * P:(c + 1) * P], ident[:])
                ins.then_inc(xT_full, 1)
        pe.wait_ge(xT_lo, NW * MC)

        def chunk(kind, head_slot, pair_slot):
            for c in range(2):
                if kind[0] in "qk":
                    n, w = "qk".index(kind[0]), int(kind[1])
                    ins = three(pe, C_ps[:], [w_qk[a][head_slot][:, n, c] for a in range(2)],
                                [xT[a][:, c, w * W:(w + 1) * W] for a in range(2)], c == 0, c == 1)
                elif kind[0] == "o":
                    m, w = int(kind[1]), int(kind[2])
                    ins = three(pe, C_ps[:], [w_o[a][:, c, m * P:(m + 1) * P] for a in range(2)],
                                [OT[a][c][:, w * W:(w + 1) * W] for a in range(2)], c == 0, c == 1)
            if kind[0] == "v":
                for a in range(2):
                    t = 2 * int(kind[1]) + a
                    for c in range(2):
                        ins = three(pe, C_ps[:, a * M:(a + 1) * M],
                                    [xT[b][:, c, t * P:(t + 1) * P] for b in range(2)],
                                    [w_v[b][:, c].rearrange("p a b -> p (a b)") for b in range(2)],
                                    c == 0, c == 1)
            ins.then_inc(chunk_full, 1)

        def scores(f, fs, i):
            s, w = fs % 2, (i + 1) * P
            need(pe, roped, 4 * f + (2 if i < GT else 4))
            need(pe, probs_ready, NT * f + i - 1)
            q = [QT[a][s][:, i * P:(i + 1) * P] for a in range(2)]
            spans = [(a, min(a + W, w)) for a in range(0, w, W)]
            for a, b in spans:
                pe.matmul(S_ps[i % 2][:, a:b], q[0], KT[0][s][:, a:b], start=True, stop=False)
                pe.matmul(S_ps[i % 2][:, a:b], q[0], KT[1][s][:, a:b], start=False, stop=False)
            for a, b in spans:
                pe.matmul(S_ps[i % 2][:, a:b], q[1], KT[0][s][:, a:b], start=False, stop=b < w)
            pe.matmul(S_ps[i % 2][:, w - P:w], ident_b[:], mask[:], start=False, stop=True
                      ).then_inc(scores_full, 1)

        def step(f, p, fs, i):
            at = f if isinstance(f, int) else 1
            if at < H:
                scores(f, fs, i)
            ch = chunk_at(f, p, fs, i)
            if ch:
                kind, number, act_no = ch
                pe.wait_ge(chunk_dve, number - 1)
                pe.wait_ge(chunk_act, act_no - (kind[0] != "o"))
                if kind[0] in "qk":
                    pe.wait_ge(qk_split, f + 2)
                elif kind[0] == "v":
                    pe.wait_ge(v_split, p + 2)
                else:
                    pe.wait_ge(o_split, p)
                    pe.wait_ge(o_parted, 2 * f - 1 + int(kind[2]))
                chunk(kind, (fs + 1) % 2, (fs // 2 + 1) % 2)
            if turned_at(at, i):
                tile = i - 1 if i else NT - 1
                pe.wait_ge(probs_ready, NT * f + i)
                for k, j, part in TURNS[i]:
                    if k - 2 in SPREAD.values():
                        need(pe, turn_hi, event_no(f, k - 2))
                    else:
                        need(pe, turn_lo, turn_no(f, j - (1 if k == 4 or k == 10 else 2)))
                    n = min(GT, tile + 1 - GT * part)
                    for a in range(n):
                        kt = GT * part + a
                        ins = pe.transpose(turn_ps[k % 2][:, a * P:(a + 1) * P],
                                           probs[:, tile % 2, kt * P:(kt + 1) * P], ident[:])
                    ins.then_inc(turn_full, 1)
            if i == 5 and at < H or i == 1 and at > 0:
                g = 0 if i == 5 else 1
                k, n = SPREAD[i], 2 * f + (1 if i == 5 else 0)
                pe.wait_ge(turn_lo, turn_no(f, 6 if i == 5 else 1))
                pe.wait_ge(recip_ready, n)
                for a in range(GT):
                    col = recip[:, g * GT + a:g * GT + a + 1]
                    ins = pe.transpose(turn_ps[k % 2][:, a * P:(a + 1) * P], col.to_broadcast([P, P]), ident[:])
                ins.then_inc(turn_full, 1)
                hs = fs if i == 5 else fs - 1
                need(pe, o_scaled, n - 1)
                pe.wait_ge(turn_lo, turn_no(f, 5 if i == 5 else 1))
                if at == 0:
                    pe.wait_ge(chunk_dve, 8)
                elif i == 5:
                    pe.wait_ge(chunk_dve, 16 * p + 4)
                last = GT * (g + 1) - 1
                for j in range(last + 1):
                    a = max(0, j - GT * g) * P
                    ins = three(pe, O_ps[:, a:W],
                                [V[b][(hs // 2) % 2][:, j, (hs % 2) * D:(hs % 2 + 1) * D] for b in range(2)],
                                [PT[b][g][:, j, a:W] for b in range(2)], j == 0, j == last)
                ins.then_inc(values_full, 1)

        for n, kind in enumerate(["q0", "k0", "q1", "k1", "v0", "v1", "v2", "v3"]):
            need(pe, chunk_dve, n)
            need(pe, chunk_act, n)
            if n == 0:
                pe.wait_ge(qk_split, 1)
            if n == 4:
                pe.wait_ge(v_split, 1)
            chunk(kind, 0, 0)
        attend_walk(pe, step)
        for n in range(4):
            kind = ["o00", "o10", "o01", "o11"][n]
            pe.wait_ge(chunk_dve, 8 * (H - 1) + 4 + n)
            pe.wait_ge(o_split, H // 2)
            pe.wait_ge(o_parted, 2 * H - 1 + int(kind[2]))
            chunk(kind, 0, 0)


def unit_walk(eng, unit):
    for n in range(3):
        unit(0, n)
    with eng.Fori(0, 6) as it:
        for n in range(3, 7):
            unit(it, n)
    for n in range(3, (E + NS) * NW - 24):
        unit(6, n)


def experts(nc, ctx, x, router_w, router_b, wu, wg, wd, su, sg, sd, r_acc, out):
    def sb(name, shape, dt=F32):
        return ctx.enter_context(nc.sbuf_tensor(name, shape, dt))

    def sem(name):
        return ctx.enter_context(nc.semaphore(name))

    NE = E + NS
    UNITS = NE * NW
    ident = sb("ident_f", [P, P])
    x1 = sb("x1", [P, NT, M])
    y = sb("y", [P, NT, M])
    xT = [sb(f"x1T{n}", [P, MC, T], F32R) for n in range(2)]
    rw = sb("rw", [E, M])
    rwT = [sb(f"rwT{n}", [P, MC, E], F32R) for n in range(2)]
    bias = sb("bias", [P, E])
    iota_i = sb("iota_i", [P, E], mybir.dt.int32)
    iota = sb("iota", [P, E])
    logits = sb("logits", [P, NT, E])
    biased = sb("biased", [P, NT, E])
    top = sb("top", [P, NT, 8])
    top_i = sb("top_i", [P, NT, 8], U32)
    top_f = sb("top_f", [P, NT, 8])
    chosen = sb("chosen", [P, 2, NT, E])
    score = sb("score", [P, NT, E])
    combine = sb("combine", [P, NT, E])
    picked = [sb(f"picked{s}", [P, NT]) for s in range(2)]
    small = sb("small", [P, 8, NT])
    stats = sb("stats", [P, NT, 6])
    mean_var = sb("mean_var", [P, NT, 2])
    raw_ug = [sb(f"raw_ug{s}", [P, 2, MC, F]) for s in range(2)]
    raw_d = [sb(f"raw_d{s}", [P, M]) for s in range(2)]
    w_ug = [[sb(f"w_ug{n}{s}", [P, 2, MC, F], F32R) for s in range(2)] for n in range(2)]
    w_d = [[sb(f"w_d{n}{s}", [P, M], F32R) for s in range(2)] for n in range(2)]
    silu = [sb(f"silu{s}", [P, W]) for s in range(2)]
    gated = [sb(f"gated{s}", [P, W]) for s in range(2)]
    hidden = [[sb(f"hidden{n}{s}", [P, W], F32R) for s in range(2)] for n in range(2)]
    yT = sb("yT", [P, MC, T])

    def ps(name):
        return ctx.enter_context(nc.psum_tensor(name, [P, W], F32))

    Y_ps = [[ps(f"Y{m}{w}") for w in range(NW)] for m in range(MC)]
    U_ps, G_ps, B_ps = [ps("U0"), ps("U1")], ps("G"), ps("B")
    banks = [U_ps[0], U_ps[1], G_ps, B_ps]

    x_in, router_in = [sem(f"x1_in{t}") for t in range(NT)], sem("router_in")
    ug_in = [sem("ug_in0"), sem("ug_in1")]
    ident_zero, ident_ready, iota_ready = sem("ident_zero"), sem("ident_ready"), sem("iota_ready")
    r_turned = sem("r_turned")
    dve_step = sem("dve_step")
    var_ready = sem("var_ready")
    dev_ready = sem("dev_ready")
    x1_ready = sem("x1_ready")
    x1_turned = sem("x1_turned")
    x1T_hi, x1T_lo = sem("x1T_hi"), sem("x1T_lo")
    rw_turned, rw_ready = sem("rw_turned"), sem("rw_ready")
    logits_full = sem("logits_full")
    shifted, exp_ready = sem("shifted"), sem("exp_ready")
    combine_ready = sem("combine_ready")
    picked_ready = sem("picked_ready")
    weights_hi = sem("weights_hi")
    waited = sem("waited_f")
    parted = sem("parted")
    up_full = sem("up_full")
    gate_full = sem("gate_full")
    down_full = sem("down_full")
    silu_ready = sem("silu_ready")
    product_ready = sem("product_ready")
    gated_ready = sem("gated_ready")
    hid_hi, hid_lo = sem("hid_hi"), sem("hid_lo")
    y_copied, y_turned, y_ready = sem("y_copied"), sem("y_turned"), sem("y_ready")
    out_done = sem("out_done")
    block = ctx.enter_context(nc.Block())

    @block.sync
    def _(sp):
        for t in range(NT):
            sp.dma_start(x1[:, t], x[0, t * P:(t + 1) * P, :]).then_inc(x_in[t], 16)
        sp.dma_start(rw[:], router_w).then_inc(router_in, 16)
        sp.dma_start(bias[:], router_b.rearrange("(o e) -> o e", o=1).to_broadcast([P, E])
                     ).then_inc(router_in, 16)

        def load(e, slot):
            if isinstance(e, int) and e >= E:
                cols = slice((e - E) * F, (e - E + 1) * F)
                up, gate, down = su[0:1, :, cols], sg[0:1, :, cols], sd[0:1, cols, :]
            else:
                up, gate, down = (w[bass.ds(e, 1)] for w in (wu, wg, wd))
            for n, w in ((0, up), (1, gate)):
                sp.dma_start(raw_ug[slot][:, n], w.rearrange("o (c p) f -> p (o c) f", p=P)
                             ).then_inc(ug_in[slot], 16)
            sp.dma_start(raw_d[slot][:], down.rearrange("o f m -> (o f) m")).then_inc(ug_in[slot], 16)

        def unit(it, n):
            e = 2 * it + n // 2
            if n % 2 == 1 and not (isinstance(e, int) and e + 2 >= NE):
                sp.wait_ge(parted, e + 1)
                load(e + 2, (n // 2) % 2)

        load(0, 0)
        load(1, 1)
        unit_walk(sp, unit)
        for t in range(NT):
            sp.wait_ge(y_ready, t + 1)
            sp.dma_start(out[0, t * P:(t + 1) * P, :], y[:, t]).then_inc(out_done, 16)
        sp.wait_ge(out_done, 16 * NT)

    @block.gpsimd
    def _(pool):
        nc.gpsimd.memset(ident[:], 0.0).then_inc(ident_zero, 1)
        pool.wait_ge(ident_zero, 1)
        nc.gpsimd.affine_select(out=ident[:], in_=ident[:], compare_op=ALU.not_equal, fill=1.0, base=0,
                                pattern=[[-1, P]], channel_multiplier=1).then_inc(ident_ready, 1)
        nc.gpsimd.iota(iota_i[:], pattern=[[1, E]], base=0, channel_multiplier=0).then_inc(iota_ready, 1)

        def part(e, turn, slot):
            pool.wait_ge(ug_in[slot], 48 * (turn + 1))
            pool.sem_inc(waited, 1)
            nc.gpsimd.tensor_copy(w_ug[0][slot][:], raw_ug[slot][:]).then_inc(weights_hi, 1)
            nc.gpsimd.tensor_copy(w_d[0][slot][:], raw_d[slot][:]).then_inc(weights_hi, 1)
            pool.wait_ge(weights_hi, 2 * e + 2)
            nc.gpsimd.tensor_tensor(w_ug[1][slot][:], raw_ug[slot][:], w_ug[0][slot][:].bitcast(F32),
                                    ALU.subtract)
            nc.gpsimd.tensor_tensor(w_d[1][slot][:], raw_d[slot][:], w_d[0][slot][:].bitcast(F32),
                                    ALU.subtract).then_inc(parted, 1)

        def unit(it, n):
            u, e = 4 * it + n, 2 * it + n // 2
            if n % 2 == 1 and not (isinstance(e, int) and e + 1 >= NE):
                need(pool, down_full, u - 1)
                part(e + 1, it + (n // 2 + 1) // 2, (n // 2 + 1) % 2)
            pool.wait_ge(hid_hi, u + 1)
            nc.gpsimd.tensor_tensor(hidden[1][n % 2][:], gated[n % 2][:], hidden[0][n % 2][:].bitcast(F32),
                                    ALU.subtract).then_inc(hid_lo, 1)

        part(0, 0, 0)
        unit_walk(pool, unit)

    @block.scalar
    def _(act):
        act.wait_ge(var_ready, 1)
        nc.scalar.activation(small[:, 1], small[:, 0], ACT.Sqrt).then_inc(dev_ready, 1)
        for n in range(MC * NW):
            w, c = n // MC, n % MC
            act.wait_ge(x1_turned, n + 1)
            nc.scalar.activation(xT[0][:, c, w * W:(w + 1) * W], Y_ps[c][w][:], ACT.Copy).then_inc(x1T_hi, 1)
        act.wait_ge(shifted, 1)
        nc.scalar.activation(score[:], score[:], ACT.Exp).then_inc(exp_ready, 1)

        def unit(it, n):
            u = 4 * it + n
            act.wait_ge(up_full, u + 1)
            need(act, gated_ready, u - 1)
            nc.scalar.activation(silu[n % 2][:], U_ps[n % 2][:], ACT.Silu).then_inc(silu_ready, 1)
            act.wait_ge(gated_ready, u + 1)
            need(act, down_full, u - 1)
            nc.scalar.activation(hidden[0][n % 2][:], gated[n % 2][:], ACT.Copy).then_inc(hid_hi, 1)

        unit_walk(act, unit)
        act.wait_ge(down_full, UNITS)
        for w in range(NW):
            for m in range(MC):
                nc.scalar.activation(yT[:, m, w * W:(w + 1) * W], Y_ps[m][w][:], ACT.Copy).then_inc(y_copied, 1)
        act.wait_ge(var_ready, 2)
        nc.scalar.activation(small[:, 1], small[:, 0], ACT.Sqrt).then_inc(dev_ready, 1)

    @block.vector
    def _(dve):
        steps = [0]

        def ordered(ins):
            steps[0] += 1
            ins.then_inc(dve_step, 1)
            dve.wait_ge(dve_step, steps[0])

        def add_and_norm(src, dst, turned, ready, which):
            for b in range(NT // 2):
                dve.wait_ge(turned, b + 1)
                if which == 1:
                    dve.wait_ge(x_in[2 * b], 16)
                    dve.wait_ge(x_in[2 * b + 1], 16)
                both = slice(2 * b, 2 * b + 2)
                ordered(nc.vector.tensor_tensor(dst[:, both].rearrange("p t m -> p (t m)"), banks[b][:],
                                                src[:, both].rearrange("p t m -> p (t m)"), ALU.add))
                for t in range(2 * b, 2 * b + 2):
                    ins = nc.vector.bn_stats(stats[:, t], dst[:, t])
                ordered(ins)
            for t in range(NT):
                ins = nc.vector.bn_aggr(mean_var[:, t], stats[:, t])
            ordered(ins)
            nc.vector.tensor_scalar(small[:, 0], mean_var[:, :, 1], EPS, None, ALU.add).then_inc(var_ready, 1)
            dve.wait_ge(dev_ready, which)
            ordered(nc.vector.reciprocal(small[:, 2], small[:, 1]))
            ordered(nc.vector.tensor_tensor(small[:, 3], small[:, 2], small[:, 0], ALU.mult))
            ordered(nc.vector.tensor_tensor(small[:, 4], small[:, 3], small[:, 1], ALU.add))
            ordered(nc.vector.tensor_scalar(small[:, 5], small[:, 4], 0.5, None, ALU.mult))
            ordered(nc.vector.reciprocal(small[:, 6], small[:, 5]))
            for t in range(NT):
                nc.vector.tensor_scalar(dst[:, t], dst[:, t], mean_var[:, t, 0:1], small[:, 6, t:t + 1],
                                        ALU.subtract, ALU.mult).then_inc(ready, 1)

        add_and_norm(x1, x1, r_turned, x1_ready, 1)
        for n in range(MC * NW):
            w, c = n // MC, n % MC
            cols = slice(w * W, (w + 1) * W)
            dve.wait_ge(x1T_hi, n + 1)
            nc.vector.tensor_tensor(xT[1][:, c, cols], Y_ps[c][w][:], xT[0][:, c, cols].bitcast(F32),
                                    ALU.subtract).then_inc(x1T_lo, 1)
        dve.wait_ge(rw_turned, 1)
        turned = banks[0][:, 0:MC * E].rearrange("p (c e) -> p c e", c=MC)
        ordered(nc.vector.tensor_copy(rwT[0][:], turned))
        nc.vector.tensor_tensor(rwT[1][:], turned, rwT[0][:].bitcast(F32), ALU.subtract).then_inc(rw_ready, 1)
        per_token = lambda a: a.unsqueeze(2).to_broadcast([P, NT, E])
        per_expert = lambda a: a.unsqueeze(1).to_broadcast([P, NT, E])
        dve.wait_ge(logits_full, 1)
        dve.wait_ge(router_in, 32)
        dve.wait_ge(iota_ready, 1)
        got = banks[1][:, 0:NT * E].rearrange("p (t e) -> p t e", t=NT)
        nc.vector.tensor_copy(iota[:], iota_i[:])
        nc.vector.tensor_copy(logits[:], got)
        ordered(nc.vector.tensor_tensor(biased[:], got, per_expert(bias[:]), ALU.add))
        nc.vector.tensor_reduce(small[:, 0], logits[:], AX.X, ALU.max)
        for t in range(NT):
            ins = nc.vector.max(top[:, t], biased[:, t])
        ordered(ins)
        nc.vector.tensor_tensor(score[:], logits[:], per_token(small[:, 0]), ALU.subtract).then_inc(shifted, 1)
        for t in range(NT):
            ins = nc.vector.max_index(top_i[:, t], top[:, t], biased[:, t])
        ordered(ins)
        ordered(nc.vector.tensor_copy(top_f[:], top_i[:]))
        for k in range(2):
            ins = nc.vector.tensor_tensor(chosen[:, k], per_expert(iota[:]), per_token(top_f[:, :, k]),
                                          ALU.is_equal)
        ordered(ins)
        ordered(nc.vector.tensor_tensor(chosen[:, 0], chosen[:, 0], chosen[:, 1], ALU.add))
        dve.wait_ge(exp_ready, 1)
        ordered(nc.vector.tensor_reduce(small[:, 1], score[:], AX.X, ALU.add))
        ordered(nc.vector.reciprocal(small[:, 2], small[:, 1]))
        ordered(nc.vector.tensor_tensor(score[:], score[:], per_token(small[:, 2]), ALU.mult))
        ordered(nc.vector.tensor_tensor(score[:], score[:], chosen[:, 0], ALU.mult))
        ordered(nc.vector.tensor_reduce(small[:, 3], score[:], AX.X, ALU.add))
        ordered(nc.vector.reciprocal(small[:, 4], small[:, 3]))
        nc.vector.tensor_tensor(combine[:], score[:], per_token(small[:, 4]), ALU.mult).then_inc(combine_ready, 1)

        def pick(e, slot):
            nc.vector.tensor_copy(picked[slot][:], combine[:, :, bass.ds(e, 1)].rearrange("p t o -> p (t o)")
                                  ).then_inc(picked_ready, 1)

        dve.wait_ge(combine_ready, 1)
        pick(0, 0)

        def unit(it, n):
            u, e, s = 4 * it + n, 2 * it + n // 2, n % 2
            shared = isinstance(u, int) and u >= E * NW
            dve.wait_ge(silu_ready, u + 1)
            dve.wait_ge(gate_full, u + 1)
            need(dve, hid_lo, u - 1)
            dst = gated[s] if shared else silu[s]
            ins = nc.vector.tensor_tensor(dst[:], G_ps[:], silu[s][:], ALU.mult)
            if not shared:
                ins.then_inc(product_ready, 1)
                dve.wait_ge(product_ready, u + 1)
                ins = nc.vector.tensor_tensor(gated[s][:], B_ps[:], silu[s][:], ALU.mult)
            ins.then_inc(gated_ready, 1)
            if s == 0 and not (isinstance(e, int) and e + 1 >= E):
                pick(e + 1, (n // 2 + 1) % 2)

        unit_walk(dve, unit)
        add_and_norm(x1, y, y_turned, y_ready, 2)

    @block.tensor
    def _(pe):
        pe.wait_ge(ident_ready, 1)

        def turn_back(src, turned, copied):
            for b in range(NT // 2):
                if copied:
                    pe.wait_ge(y_copied, MC * (b // 2 + 1))
                for t in range(2 * b, 2 * b + 2):
                    for c in range(MC):
                        ins = pe.transpose(banks[b][:, (t % 2) * M + c * P:(t % 2) * M + (c + 1) * P],
                                           src[:, c, t * P:(t + 1) * P], ident[:])
                ins.then_inc(turned, 1)

        turn_back(r_acc, r_turned, False)
        for w in range(NW):
            pe.wait_ge(x1_ready, GT * (w + 1))
            for c in range(MC):
                for a in range(GT):
                    ins = pe.transpose(Y_ps[c][w][:, a * P:(a + 1) * P],
                                       x1[:, w * GT + a, c * P:(c + 1) * P], ident[:])
                ins.then_inc(x1_turned, 1)
        pe.wait_ge(router_in, 32)
        for c in range(MC):
            ins = pe.transpose(banks[0][:, c * E:(c + 1) * E], rw[:, c * P:(c + 1) * P], ident[0:E, 0:E])
        ins.then_inc(rw_turned, 1)
        pe.wait_ge(x1T_lo, MC * NW)
        pe.wait_ge(rw_ready, 1)
        for t in range(NT):
            for c in range(MC):
                ins = three(pe, banks[1][:, t * E:(t + 1) * E], [xT[a][:, c, t * P:(t + 1) * P] for a in range(2)],
                            [rwT[a][:, c] for a in range(2)], c == 0, c == MC - 1)
        ins.then_inc(logits_full, 1)

        def down(v, n):
            s, e, w = n % 2, n // 2, n % 2
            pe.wait_ge(hid_lo, v + 1)
            first = isinstance(v, int) and v < NW
            last = isinstance(v, int) and v >= UNITS - NW
            for m in range(MC):
                ins = three(pe, Y_ps[m][w][:], [w_d[a][e % 2][:, m * P:(m + 1) * P] for a in range(2)],
                            [hidden[a][s][:] for a in range(2)], first, last)
            ins.then_inc(down_full, 1)

        def unit(it, n):
            u, e, slot, w = 4 * it + n, 2 * it + n // 2, (n // 2) % 2, n % 2
            shared = isinstance(u, int) and u >= E * NW
            pe.wait_ge(parted, e + 1)
            if isinstance(u, int) and u == 1:
                pe.wait_ge(combine_ready, 1)
            need(pe, silu_ready, u - 1)
            for g, bank in ((0, U_ps[n % 2]), (1, G_ps)):
                if g == 1:
                    need(pe, gated_ready, u)
                for c in range(MC):
                    ins = three(pe, bank[:], [w_ug[a][slot][:, g, c] for a in range(2)],
                                [xT[a][:, c, w * W:(w + 1) * W] for a in range(2)], c == 0, c == MC - 1)
                if g == 0:
                    ins.then_inc(up_full, 1)
            if not shared:
                pe.wait_ge(picked_ready, e + 1)
                for a in range(GT):
                    col = picked[slot][:, w * GT + a:w * GT + a + 1]
                    ins = pe.transpose(B_ps[:, a * P:(a + 1) * P], col.to_broadcast([P, P]), ident[:])
            ins.then_inc(gate_full, 1)
            if not (isinstance(u, int) and u == 0):
                down(u - 1, n - 1 if n else 0)

        unit_walk(pe, unit)
        down(UNITS - 1, UNITS - 1 - 24)
        turn_back(yT, y_turned, True)


_INS = ['L0_attn_x', 'L0_attn_w_aq', 'L0_attn_w_ak', 'L0_attn_w_av', 'L0_attn_w_ao', 'L0_ffn_router_w',
        'L0_ffn_router_bias', 'L0_ffn_Wu', 'L0_ffn_Wg', 'L0_ffn_Wd', 'L0_ffn_Su', 'L0_ffn_Sg', 'L0_ffn_Sd']


def layer(nc, x, wq, wk, wv, wo, router_w, router_b, wu, wg, wd, su, sg, sd, cos_t, sin_t, out):
    with nc.sbuf_tensor("r_acc", [P, MC, T], F32) as r_acc:
        with ExitStack() as ctx:
            attention(nc, ctx, x, wq, wk, wv, wo, cos_t, sin_t, r_acc)
        with ExitStack() as ctx:
            experts(nc, ctx, x, router_w, router_b, wu, wg, wd, su, sg, sd, r_acc, out)


def rotary_tables():
    freqs = np.power(float(ROTARY_BASE), -np.arange(D // 2) / (D // 2)).astype(np.float32)
    angles = (np.arange(T, dtype=np.float32)[None, :] * freqs[:, None]).astype(np.float32)
    cos, sin = np.cos(angles.astype(np.float64)), np.sin(angles.astype(np.float64))
    return (np.concatenate([cos, cos]).astype(np.float32), np.concatenate([-sin, sin]).astype(np.float32))


def kernel(**inputs):
    import concourse.bacc as _bacc
    from concourse.bass_utils import run_bass_kernel_spmd as _run

    nc = _bacc.Bacc("TRN2", target_bir_lowering=False, num_devices=1)
    arrays, args = {}, []
    for name in _INS:
        arrays[name] = np.ascontiguousarray(inputs[name])
    arrays["cos_t"], arrays["sin_t"] = rotary_tables()
    for name, a in arrays.items():
        args.append(nc.dram_tensor(name, a.shape, mybir.dt.from_np(a.dtype), kind="ExternalInput").ap())
    args.append(nc.dram_tensor("out", (1, T, M), F32, kind="ExternalOutput").ap())
    layer(nc, *args)
    return _run(nc, [arrays], core_ids=[0]).results[0]["out"]
```

```python
from contextlib import ExitStack

import numpy as np

import concourse.bass as bass
from concourse import mybir

F32 = mybir.dt.float32
F32R = mybir.dt.float32r
BF16 = mybir.dt.bfloat16
U32 = mybir.dt.uint32
ALU = mybir.AluOpType
ACT = mybir.ActivationFunctionType
AX = mybir.AxisListType

P = 128
T, M = 1024, 256
H, D = 16, 128
E, F = 16, 128
NS = 2
MC = M // P
NT = T // P
W = 512
NW = T // W
GT = W // P
EPS = 1e-5
MASKED = -1e30
ROTARY_BASE = 1250

TURNS = {0: [(0, 0, 0), (1, 1, 1)], 1: [(3, 2, 0)], 2: [(4, 3, 0)], 3: [(5, 4, 0)], 4: [(6, 5, 0)],
         5: [(8, 6, 0), (9, 7, 1)], 6: [(10, 8, 0), (11, 9, 1)], 7: [(12, 10, 0), (13, 11, 1)]}
SPREAD = {1: 2, 5: 7}
NEVENT, NTURN = 14, 12


def need(eng, sem, count):
    if not isinstance(count, int) or count > 0:
        eng.wait_ge(sem, count)


def event_no(f, k):
    if isinstance(f, int) and f <= 0:
        return max(0, k - 2) if f == 0 else 0
    return NEVENT * f + k - 2


def turn_no(f, j):
    return NTURN * f + j - 1


def three(eng, out, a, b, start, stop):
    eng.matmul(out, a[0], b[0], start=start, stop=False)
    eng.matmul(out, a[0], b[1], start=False, stop=False)
    return eng.matmul(out, a[1], b[0], start=False, stop=stop)


def turned_at(f, i):
    return (f, i) not in ((0, 0), (H, 1))


def rotation_no(f, kind):
    return 4 * f + 5 + ["q0", "k0", "q1", "k1"].index(kind)


def attend_walk(eng, step):
    for i in range(NT):
        step(0, 0, 0, i)
    with eng.Fori(0, 3) as it:
        for s in range(NT, 5 * NT):
            step(4 * it + s // NT, 2 * it + s // NT // 2, s // NT, s % NT)
    for s in range(13 * NT, H * NT):
        step(s // NT, s // NT // 2, s // NT, s % NT)
    step(H, H // 2, H, 0)
    step(H, H // 2, H, 1)


def chunk_at(f, p, fs, i):
    first, last = isinstance(f, int) and f == 0, isinstance(f, int) and f == H - 1
    if last or isinstance(f, int) and f == H:
        return None
    if fs % 2 == 0:
        kind = ["q0", "o00", "k0", "o10", "q1", "o01", "k1", "o11"][i]
        if kind[0] == "o" and first:
            return None
        return kind, (9 + i // 2 if first else 8 * f + 5 + i), 12 * p + 9 + i // 2
    return ["q0", "v0", "k0", "v1", "q1", "v2", "k1", "v3"][i], 8 * f + 5 + i, 12 * p + 13 + i


def attention(nc, ctx, x, wq, wk, wv, wo, cos_t, sin_t, r_acc):
    def sb(name, shape, dt=F32):
        return ctx.enter_context(nc.sbuf_tensor(name, shape, dt))

    def sem(name):
        return ctx.enter_context(nc.semaphore(name))

    xT = [sb("xT_hi", [P, MC, T], F32R), sb("xT_lo", [P, MC, T], F32R)]
    cos = sb("cos", [P, T])
    sin = sb("sin", [P, T])
    ident = sb("ident_a", [P, P])
    ident_b = sb("ident_b", [P, P], BF16)
    mask = sb("mask", [P, P], BF16)
    raw_qk = [sb(f"raw_qk{s}", [P, 2, MC, D]) for s in range(2)]
    raw_v = sb("raw_v", [P, MC, 2, D])
    raw_o = sb("raw_o", [P, 2, M])
    w_qk = [[sb(f"w_qk{n}{s}", [P, 2, MC, D], F32R) for s in range(2)] for n in range(2)]
    w_v = [sb(f"w_v{n}", [P, MC, 2, D], F32R) for n in range(2)]
    w_o = [sb(f"w_o{n}", [P, 2, M], F32R) for n in range(2)]
    swapped = [sb(f"swapped{s}", [P, W]) for s in range(2)]
    rotated = [sb(f"rotated{s}", [P, W]) for s in range(2)]
    QT = [[sb(f"QT{n}{s}", [P, T], F32R) for s in range(2)] for n in range(2)]
    KT = [[sb(f"KT{n}{s}", [P, T], F32R) for s in range(2)] for n in range(2)]
    V = [[sb(f"V{n}{s}", [P, NT, 2 * D], F32R) for s in range(2)] for n in range(2)]
    probs = sb("probs", [P, 2, T])
    PT = [[sb(f"PT{n}{g}", [P, GT * (g + 1), W], F32R) for g in range(2)] for n in range(2)]
    spread = sb("spread", [P, W])
    o_buf = sb("o_buf", [P, W])
    OT = [[sb(f"OT{n}{s}", [P, T], F32R) for s in range(2)] for n in range(2)]
    neg_max = sb("neg_max", [P, NT])
    row_sum = sb("row_sum", [P, NT])
    recip = sb("recip", [P, NT])
    x_tok = probs[:].rearrange("p s (t m) -> p (s t) m", m=M)

    S_ps = [ctx.enter_context(nc.psum_tensor(f"S{s}", [P, T], F32)) for s in range(2)]
    turn_ps = [ctx.enter_context(nc.psum_tensor(f"turn{s}", [P, W], F32)) for s in range(2)]
    O_ps = ctx.enter_context(nc.psum_tensor("O", [P, W], F32))
    C_ps = ctx.enter_context(nc.psum_tensor("C", [P, W], F32))

    x_in = [sem(f"x_in{t}") for t in range(NT)]
    tables_in = sem("tables_in")
    qk_in = [sem("qk_in0"), sem("qk_in1")]
    v_in, o_in = sem("v_in"), sem("o_in")
    zeroed, consts = sem("zeroed"), sem("consts")
    xT_full, xT_hi, xT_lo = sem("xT_full"), sem("xT_hi"), sem("xT_lo")
    qk_split, v_split, o_split = sem("qk_split"), sem("v_split"), sem("o_split")
    scores_full = sem("scores_full")
    chunk_full = sem("chunk_full")
    turn_full = sem("turn_full")
    values_full = sem("values_full")
    max_ready = sem("max_ready")
    probs_ready = sem("probs_ready")
    turn_hi = sem("turn_hi")
    turn_lo = sem("turn_lo")
    chunk_act = sem("chunk_act")
    chunk_dve = sem("chunk_dve")
    recip_ready = sem("recip_ready")
    o_scaled = sem("o_scaled")
    o_hi = sem("o_hi")
    o_parted = sem("o_parted")
    sin_done = sem("sin_done")
    rope_sum = sem("rope_sum")
    rope_hi = sem("rope_hi")
    roped = sem("roped")
    qk_hi, v_hi, o_w_hi = sem("qk_hi"), sem("v_hi"), sem("o_w_hi")

    def chunk_bank(i):
        return {1: S_ps[0][:, W:T], 3: S_ps[1][:, W:T]}.get(i, C_ps[:])

    block = ctx.enter_context(nc.Block())

    @block.sync
    def _(sp):
        sp.dma_start(raw_qk[0][:, 0], wq[0].rearrange("(c p) d -> p c d", p=P)).then_inc(qk_in[0], 16)
        sp.dma_start(raw_qk[0][:, 1], wk[0].rearrange("(c p) d -> p c d", p=P)).then_inc(qk_in[0], 16)
        for t in range(NT):
            sp.dma_start(x_tok[:, t], x[0, t * P:(t + 1) * P, :]).then_inc(x_in[t], 16)
        sp.dma_start(cos[:], cos_t).then_inc(tables_in, 16)
        sp.dma_start(sin[:], sin_t).then_inc(tables_in, 16)

        def load_qk(h, slot):
            for n, w in ((0, wq), (1, wk)):
                sp.dma_start(raw_qk[slot][:, n], w[bass.ds(h, 1)].rearrange("o (c p) d -> p (o c) d", p=P)
                             ).then_inc(qk_in[slot], 16)

        def load_v(pair):
            for n in range(2):
                sp.dma_start(raw_v[:, :, n], wv[bass.ds(2 * pair + n, 1)].rearrange(
                    "o (c p) d -> p (o c) d", p=P)).then_inc(v_in, 16)

        def load_o(pair):
            sp.dma_start(raw_o[:], wo[bass.ds(2 * pair, 2)].rearrange("n d m -> d n m")).then_inc(o_in, 16)

        load_v(0)
        load_qk(1, 1)
        load_o(0)
        sp.wait_ge(qk_split, 1)
        load_qk(2, 0)
        sp.wait_ge(v_split, 1)
        load_v(1)

        def frame(f, p, fs):
            last = f if isinstance(f, int) else 0
            if last + 3 < H:
                sp.wait_ge(qk_split, f + 2)
                load_qk(f + 3, (fs + 3) % 2)
            if fs % 2 == 1:
                if last // 2 + 2 < H // 2:
                    sp.wait_ge(v_split, p + 2)
                    load_v(p + 2)
                if last // 2 + 1 < H // 2:
                    sp.wait_ge(o_split, p + 1)
                    load_o(p + 1)

        frame(0, 0, 0)
        with sp.Fori(0, 3) as it:
            for fs in range(1, 5):
                frame(4 * it + fs, 2 * it + fs // 2, fs)
        for f in range(13, H):
            frame(f, f // 2, f)

    @block.gpsimd
    def _(pool):
        nc.gpsimd.memset(ident[:], 0.0).then_inc(zeroed, 1)
        nc.gpsimd.memset(ident_b[:], 0.0).then_inc(zeroed, 1)
        nc.gpsimd.memset(mask[:], 0.0).then_inc(zeroed, 1)
        nc.gpsimd.memset(r_acc[:], 0.0).then_inc(zeroed, 1)
        pool.wait_ge(zeroed, 4)
        for m in (ident, ident_b):
            nc.gpsimd.affine_select(out=m[:], in_=m[:], compare_op=ALU.not_equal, fill=1.0, base=0,
                                    pattern=[[-1, P]], channel_multiplier=1).then_inc(consts, 1)
        nc.gpsimd.affine_select(out=mask[:], in_=mask[:], compare_op=ALU.is_ge, fill=MASKED, base=0,
                                pattern=[[-1, P]], channel_multiplier=1).then_inc(consts, 1)

        def low(raw, hi, lo, hi_sem, count, ready):
            pool.wait_ge(hi_sem, count)
            nc.gpsimd.tensor_tensor(lo, raw, hi.bitcast(F32), ALU.subtract).then_inc(ready, 1)

        def low_qk(h, slot):
            low(raw_qk[slot][:], w_qk[0][slot][:], w_qk[1][slot][:], qk_hi, h + 1, qk_split)

        def low_v(pair):
            low(raw_v[:], w_v[0][:], w_v[1][:], v_hi, pair + 1, v_split)

        def low_o(pair):
            low(raw_o[:], w_o[0][:], w_o[1][:], o_w_hi, pair + 1, o_split)

        def rotate(kind, number, act_no, dve_no):
            slot, half = "qk".index(kind[0]), int(kind[1])
            pool.wait_ge(chunk_act, act_no)
            nc.gpsimd.tensor_tensor(swapped[slot][:], swapped[slot][:], sin[:, half * W:(half + 1) * W],
                                    ALU.mult).then_inc(sin_done, 1)
            pool.wait_ge(chunk_dve, dve_no)
            pool.wait_ge(sin_done, number)
            nc.gpsimd.tensor_tensor(rotated[slot][:], rotated[slot][:], swapped[slot][:], ALU.add
                                    ).then_inc(rope_sum, 1)

        def low_rotated(kind, dst, number):
            cols = slice(int(kind[1]) * W, (int(kind[1]) + 1) * W)
            bufs = QT if kind[0] == "q" else KT
            low(rotated["qk".index(kind[0])][:], bufs[0][dst][:, cols], bufs[1][dst][:, cols],
                rope_hi, number, roped)

        def low_out(f, fs, g):
            cols = slice(g * W, (g + 1) * W)
            low(o_buf[:], OT[0][fs % 2][:, cols], OT[1][fs % 2][:, cols], o_hi, 2 * f + g + 1, o_parted)

        def step(f, p, fs, i):
            at = f if isinstance(f, int) else 1
            if i == 2 and at > 0:
                low_out(f - 1, fs - 1, 1)
            if i == 6:
                low_out(f, fs, 0)
            ch = chunk_at(f, p, fs, i)
            if ch and ch[0][0] in "qk":
                rotate(ch[0], rotation_no(f, ch[0]), ch[2], ch[1])
            before = chunk_at(f, p, fs, i - 1) if i else None
            if before and before[0][0] in "qk":
                low_rotated(before[0], (fs + 1) % 2, rotation_no(f, before[0]))
            if i == 3 and fs % 2 == 0 and at // 2 + 1 < H // 2:
                low_v(p + 1)
            if i == 3 and fs % 2 == 1:
                low_o(p)
            if i == 5 and at + 2 < H:
                low_qk(f + 2, fs % 2)

        low_qk(0, 0)
        low_v(0)
        pool.wait_ge(tables_in, 32)
        kinds = ["q0", "k0", "q1", "k1"]
        for n, kind in enumerate(kinds):
            rotate(kind, n + 1, n + 1, n + 1)
            if n:
                low_rotated(kinds[n - 1], 0, n)
        low_rotated("k1", 0, 4)
        low_qk(1, 1)
        attend_walk(pool, step)
        low_out(H - 1, H - 1, 1)

    @block.scalar
    def _(act):
        for n in range(NW * MC):
            c, w = n // NW, n % NW
            act.wait_ge(xT_full, n + 1)
            nc.scalar.activation(xT[0][:, c, w * W:(w + 1) * W], S_ps[c][:, w * W:(w + 1) * W],
                                 ACT.Copy).then_inc(xT_hi, 1)

        def read_chunk(kind, bank, pair_slot, number, act_no, rope_no):
            act.wait_ge(chunk_full, number)
            if kind[0] in "qk":
                slot, scale = "qk".index(kind[0]), (1.0 / D if kind[0] == "q" else 1.0)
                need(act, roped, rope_no - 2)
                nc.scalar.activation(swapped[slot][0:D // 2], bank[D // 2:D, :], ACT.Copy, scale=scale)
                nc.scalar.activation(swapped[slot][D // 2:D], bank[0:D // 2, :], ACT.Copy, scale=scale
                                     ).then_inc(chunk_act, 1)
            else:
                t = 2 * int(kind[1])
                nc.scalar.activation(V[0][pair_slot][:, t:t + 2].rearrange("p a b -> p (a b)"), bank,
                                     ACT.Copy).then_inc(chunk_act, 1)

        def high_rotated(kind, dst, number):
            cols = slice(int(kind[1]) * W, (int(kind[1]) + 1) * W)
            act.wait_ge(rope_sum, number)
            nc.scalar.activation((QT if kind[0] == "q" else KT)[0][dst][:, cols],
                                 rotated["qk".index(kind[0])][:], ACT.Copy).then_inc(rope_hi, 1)

        def high_out(f, fs, g):
            act.wait_ge(o_scaled, 2 * f + g + 1)
            nc.scalar.activation(OT[0][fs % 2][:, g * W:(g + 1) * W], o_buf[:], ACT.Copy).then_inc(o_hi, 1)

        def step(f, p, fs, i):
            at = f if isinstance(f, int) else 1
            if i == 2 and at > 0:
                high_out(f - 1, fs - 1, 1)
            if i == 6:
                high_out(f, fs, 0)
            ch = chunk_at(f, p, fs, i)
            if ch and ch[0][0] != "o":
                read_chunk(ch[0], chunk_bank(i), (fs // 2 + 1) % 2, ch[1], ch[2],
                           rotation_no(f, ch[0]) if ch[0][0] in "qk" else 0)
            if i == 5 and at < H or i == 1 and at > 0:
                k = SPREAD[i]
                act.wait_ge(turn_full, event_no(f, k))
                need(act, o_scaled, 2 * f + (0 if i == 5 else -1))
                nc.scalar.activation(spread[:], turn_ps[k % 2][:], ACT.Copy).then_inc(turn_hi, 1)
            if turned_at(at, i):
                tile = i - 1 if i else NT - 1
                for k, _, part in TURNS[i]:
                    act.wait_ge(turn_full, event_no(f, k))
                    g, n = tile // GT, min(GT, tile + 1 - GT * part)
                    nc.scalar.activation(PT[0][g][:, GT * part:GT * part + n, (tile % GT) * P:(tile % GT + 1) * P],
                                         turn_ps[k % 2][:, 0:n * P].rearrange("p (a b) -> p a b", a=n),
                                         ACT.Copy).then_inc(turn_hi, 1)
            before = chunk_at(f, p, fs, i - 1) if i else None
            if before and before[0][0] in "qk":
                high_rotated(before[0], (fs + 1) % 2, rotation_no(f, before[0]))
            if at < H:
                act.wait_ge(max_ready, NT * f + i + 1)
                w = (i + 1) * P
                nc.scalar.activation(probs[:, i % 2, 0:w], S_ps[i % 2][:, 0:w], ACT.Exp,
                                     bias=neg_max[:, i:i + 1], accum_out=row_sum[:, i:i + 1]
                                     ).then_inc(probs_ready, 1)

        for n, kind in enumerate(["q0", "k0", "q1", "k1", "v0", "v1", "v2", "v3"]):
            read_chunk(kind, C_ps[:], 0, n + 1, n + 1, n + 1)
            if 1 <= n <= 4:
                high_rotated(["q0", "k0", "q1", "k1"][n - 1], 0, n)
        attend_walk(act, step)
        high_out(H - 1, H - 1, 1)

    @block.vector
    def _(dve):
        def high_first():
            dve.wait_ge(qk_in[0], 32)
            nc.vector.tensor_copy(w_qk[0][0][:], raw_qk[0][:]).then_inc(qk_hi, 1)
            dve.wait_ge(v_in, 32)
            nc.vector.tensor_copy(w_v[0][:], raw_v[:]).then_inc(v_hi, 1)

        high_first()
        for n in range(NW * MC):
            c, w = n // NW, n % NW
            dve.wait_ge(xT_hi, n + 1)
            nc.vector.tensor_tensor(xT[1][:, c, w * W:(w + 1) * W], S_ps[c][:, w * W:(w + 1) * W],
                                    xT[0][:, c, w * W:(w + 1) * W].bitcast(F32), ALU.subtract
                                    ).then_inc(xT_lo, 1)

        def read_chunk(kind, bank, pair_slot, number, act_no, rope_no):
            if kind[0] in "qk":
                slot, half = "qk".index(kind[0]), int(kind[1])
                dve.wait_ge(chunk_act, act_no)
                need(dve, roped, rope_no - 2)
                nc.vector.scalar_tensor_tensor(out=rotated[slot][:], in0=bank,
                                               scalar=1.0 / D if kind[0] == "q" else 1.0,
                                               in1=cos[:, half * W:(half + 1) * W], op0=ALU.mult,
                                               op1=ALU.mult).then_inc(chunk_dve, 1)
            elif kind[0] == "v":
                t = 2 * int(kind[1])
                dve.wait_ge(chunk_act, act_no)
                nc.vector.tensor_tensor(V[1][pair_slot][:, t:t + 2].rearrange("p a b -> p (a b)"), bank,
                                        V[0][pair_slot][:, t:t + 2].rearrange("p a b -> p (a b)").bitcast(F32),
                                        ALU.subtract).then_inc(chunk_dve, 1)
            else:
                c, w = int(kind[1]), int(kind[2])
                dve.wait_ge(chunk_full, number)
                nc.vector.tensor_tensor(r_acc[:, c, w * W:(w + 1) * W], bank,
                                        r_acc[:, c, w * W:(w + 1) * W], ALU.add).then_inc(chunk_dve, 1)

        def high_qk(h, turn, slot):
            dve.wait_ge(qk_in[slot], 32 * (turn + 1))
            nc.vector.tensor_copy(w_qk[0][slot][:], raw_qk[slot][:]).then_inc(qk_hi, 1)

        def high_v(pair):
            dve.wait_ge(v_in, 32 * (pair + 1))
            nc.vector.tensor_copy(w_v[0][:], raw_v[:]).then_inc(v_hi, 1)

        def high_o(pair):
            dve.wait_ge(o_in, 16 * (pair + 1))
            nc.vector.tensor_copy(w_o[0][:], raw_o[:]).then_inc(o_w_hi, 1)

        def reciprocals(f, g):
            dve.wait_ge(probs_ready, NT * f + GT * (g + 1))
            nc.vector.reciprocal(recip[:, g * GT:(g + 1) * GT], row_sum[:, g * GT:(g + 1) * GT]
                                 ).then_inc(recip_ready, 1)

        def step(f, p, fs, i):
            at = f if isinstance(f, int) else 1
            if at < H:
                dve.wait_ge(scores_full, NT * f + i + 1)
                nc.vector.tensor_reduce(neg_max[:, i:i + 1], S_ps[i % 2][:, 0:(i + 1) * P], AX.X, ALU.max,
                                        negate=True).then_inc(max_ready, 1)
            ch = chunk_at(f, p, fs, i)
            if ch:
                read_chunk(ch[0], chunk_bank(i), (fs // 2 + 1) % 2, ch[1], ch[2],
                           rotation_no(f, ch[0]) if ch[0][0] in "qk" else 0)
            if turned_at(at, i):
                tile = i - 1 if i else NT - 1
                for k, j, part in TURNS[i]:
                    dve.wait_ge(turn_hi, event_no(f, k))
                    g, n = tile // GT, min(GT, tile + 1 - GT * part)
                    at_ = (slice(None), slice(GT * part, GT * part + n), slice((tile % GT) * P, (tile % GT + 1) * P))
                    nc.vector.tensor_tensor(PT[1][g][at_],
                                            turn_ps[k % 2][:, 0:n * P].rearrange("p (a b) -> p a b", a=n),
                                            PT[0][g][at_].bitcast(F32), ALU.subtract).then_inc(turn_lo, 1)
            if i == 2 and fs % 2 == 0 and at // 2 + 1 < H // 2:
                dve.wait_ge(chunk_full, 8 if at == 0 else 16 * p + 4)
                high_v(p + 1)
            if i == 2 and fs % 2 == 1:
                dve.wait_ge(chunk_full, 16 * p + 12)
                high_o(p)
            if i == 4 and at + 2 < H:
                high_qk(f + 2, p + 1, fs % 2)
            if i == 0 and at > 0:
                reciprocals(f - 1, 1)
            if i == 4 and at < H:
                reciprocals(f, 0)
            if i == 5 and at < H or i == 1 and at > 0:
                n = 2 * f + (1 if i == 5 else 0)
                dve.wait_ge(values_full, n)
                dve.wait_ge(turn_hi, event_no(f, SPREAD[i]))
                need(dve, o_parted, n - 1)
                nc.vector.tensor_tensor(o_buf[:], O_ps[:], spread[:], ALU.mult).then_inc(o_scaled, 1)

        high_qk(1, 0, 1)
        dve.wait_ge(tables_in, 32)
        dve.wait_ge(zeroed, 4)
        for n, kind in enumerate(["q0", "k0", "q1", "k1", "v0", "v1", "v2", "v3"]):
            read_chunk(kind, C_ps[:], 0, n + 1, n + 1, n + 1)
        attend_walk(dve, step)
        for n in range(4):
            read_chunk(["o00", "o10", "o01", "o11"][n], C_ps[:], 0, 8 * (H - 1) + 5 + n, 0, 0)

    @block.tensor
    def _(pe):
        pe.wait_ge(consts, 3)
        for c in range(MC):
            for w in range(NW):
                for q in range(GT):
                    t = w * GT + q
                    pe.wait_ge(x_in[t], 16)
                    ins = pe.transpose(S_ps[c][:, t * P:(t + 1) * P], x_tok[:, t, c * P:(c + 1) * P], ident[:])
                ins.then_inc(xT_full, 1)
        pe.wait_ge(xT_lo, NW * MC)

        def chunk(kind, bank, head_slot, pair_slot):
            for c in range(2):
                if kind[0] in "qk":
                    n, w = "qk".index(kind[0]), int(kind[1])
                    ins = three(pe, bank, [w_qk[a][head_slot][:, n, c] for a in range(2)],
                                [xT[a][:, c, w * W:(w + 1) * W] for a in range(2)], c == 0, c == 1)
                elif kind[0] == "o":
                    m, w = int(kind[1]), int(kind[2])
                    ins = three(pe, bank, [w_o[a][:, c, m * P:(m + 1) * P] for a in range(2)],
                                [OT[a][c][:, w * W:(w + 1) * W] for a in range(2)], c == 0, c == 1)
            if kind[0] == "v":
                for a in range(2):
                    t = 2 * int(kind[1]) + a
                    for c in range(2):
                        ins = three(pe, bank[:, a * M:(a + 1) * M],
                                    [xT[b][:, c, t * P:(t + 1) * P] for b in range(2)],
                                    [w_v[b][:, c].rearrange("p a b -> p (a b)") for b in range(2)],
                                    c == 0, c == 1)
            ins.then_inc(chunk_full, 1)

        def scores(f, fs, i):
            s, w = fs % 2, (i + 1) * P
            need(pe, roped, 4 * f + (2 if i < GT else 4))
            need(pe, probs_ready, NT * f + i - 1)
            if i in (GT, GT + 1) and not (isinstance(f, int) and f in (0, H - 1)):
                pe.wait_ge(chunk_dve, chunk_at(f, 0, fs, 1 if i == GT else 3)[1])
            q = [QT[a][s][:, i * P:(i + 1) * P] for a in range(2)]
            spans = [(a, min(a + W, w)) for a in range(0, w, W)]
            for a, b in spans:
                pe.matmul(S_ps[i % 2][:, a:b], q[0], KT[0][s][:, a:b], start=True, stop=False)
                pe.matmul(S_ps[i % 2][:, a:b], q[0], KT[1][s][:, a:b], start=False, stop=False)
            for a, b in spans:
                pe.matmul(S_ps[i % 2][:, a:b], q[1], KT[0][s][:, a:b], start=False, stop=b < w)
            pe.matmul(S_ps[i % 2][:, w - P:w], ident_b[:], mask[:], start=False, stop=True
                      ).then_inc(scores_full, 1)

        def turn(f, tile, k, j, part):
            if k - 2 in SPREAD.values():
                need(pe, turn_hi, event_no(f, k - 2))
            else:
                need(pe, turn_lo, turn_no(f, j - (1 if k - 1 in SPREAD.values() else 2)))
            n = min(GT, tile + 1 - GT * part)
            for a in range(n):
                kt = GT * part + a
                ins = pe.transpose(turn_ps[k % 2][:, a * P:(a + 1) * P],
                                   probs[:, tile % 2, kt * P:(kt + 1) * P], ident[:])
            ins.then_inc(turn_full, 1)

        def step(f, p, fs, i):
            at = f if isinstance(f, int) else 1
            if at < H:
                scores(f, fs, i)
            ch = chunk_at(f, p, fs, i)
            if ch:
                kind, number, _ = ch
                if at == 0:
                    pe.wait_ge(chunk_dve, number - 1)
                elif i not in (1, 3):
                    pe.wait_ge(chunk_dve, number - (2 if i in (2, 4) else 1))
                if kind[0] in "qk":
                    pe.wait_ge(qk_split, f + 2)
                elif kind[0] == "v":
                    pe.wait_ge(v_split, p + 2)
                else:
                    pe.wait_ge(o_split, p)
                    pe.wait_ge(o_parted, 2 * f - 1 + int(kind[2]))
                chunk(kind, chunk_bank(i), (fs + 1) % 2, (fs // 2 + 1) % 2)
            valued = i == 5 and at < H or i == 1 and at > 0
            if valued:
                g, n = (0 if i == 5 else 1), 2 * f + (1 if i == 5 else 0)
                k = SPREAD[i]
                pe.wait_ge(turn_lo, turn_no(f, 4 if i == 5 else 0))
                pe.wait_ge(recip_ready, n)
                for a in range(GT):
                    col = recip[:, g * GT + a:g * GT + a + 1]
                    ins = pe.transpose(turn_ps[k % 2][:, a * P:(a + 1) * P], col.to_broadcast([P, P]), ident[:])
                ins.then_inc(turn_full, 1)
            if turned_at(at, i):
                tile = i - 1 if i else NT - 1
                pe.wait_ge(probs_ready, NT * f + i)
                turn(f, tile, *TURNS[i][0])
            if valued:
                hs = fs if i == 5 else fs - 1
                need(pe, o_scaled, n - 1)
                pe.wait_ge(turn_lo, turn_no(f, 5 if i == 5 else 1))
                if at == 0:
                    pe.wait_ge(chunk_dve, 8)
                elif i == 5:
                    pe.wait_ge(chunk_dve, 16 * p + 4)
                last = GT * (g + 1) - 1
                for j in range(last + 1):
                    a = max(0, j - GT * g) * P
                    ins = three(pe, O_ps[:, a:W],
                                [V[b][(hs // 2) % 2][:, j, (hs % 2) * D:(hs % 2 + 1) * D] for b in range(2)],
                                [PT[b][g][:, j, a:W] for b in range(2)], j == 0, j == last)
                ins.then_inc(values_full, 1)
            if turned_at(at, i) and len(TURNS[i]) > 1:
                turn(f, tile, *TURNS[i][1])

        for n, kind in enumerate(["q0", "k0", "q1", "k1", "v0", "v1", "v2", "v3"]):
            need(pe, chunk_dve, n)
            if n == 0:
                pe.wait_ge(qk_split, 1)
            if n == 4:
                pe.wait_ge(v_split, 1)
            chunk(kind, C_ps[:], 0, 0)
        attend_walk(pe, step)
        for n in range(4):
            kind = ["o00", "o10", "o01", "o11"][n]
            pe.wait_ge(chunk_dve, 8 * (H - 1) + 4 + n)
            pe.wait_ge(o_split, H // 2)
            pe.wait_ge(o_parted, 2 * H - 1 + int(kind[2]))
            chunk(kind, C_ps[:], 0, 0)


def unit_walk(eng, unit):
    for n in range(3):
        unit(0, n)
    with eng.Fori(0, 6) as it:
        for n in range(3, 7):
            unit(it, n)
    for n in range(3, (E + NS) * NW - 24):
        unit(6, n)


def experts(nc, ctx, x, router_w, router_b, wu, wg, wd, su, sg, sd, r_acc, out):
    def sb(name, shape, dt=F32):
        return ctx.enter_context(nc.sbuf_tensor(name, shape, dt))

    def sem(name):
        return ctx.enter_context(nc.semaphore(name))

    NE = E + NS
    UNITS = NE * NW
    ident = sb("ident_f", [P, P])
    x1 = sb("x1", [P, NT, M])
    y = sb("y", [P, NT, M])
    xT = [sb(f"x1T{n}", [P, MC, T], F32R) for n in range(2)]
    rw = sb("rw", [E, M])
    rwT = [sb(f"rwT{n}", [P, MC, E], F32R) for n in range(2)]
    bias = sb("bias", [P, E])
    iota_i = sb("iota_i", [P, E], mybir.dt.int32)
    iota = sb("iota", [P, E])
    logits = sb("logits", [P, NT, E])
    biased = sb("biased", [P, NT, E])
    top = sb("top", [P, NT, 8])
    top_i = sb("top_i", [P, NT, 8], U32)
    top_f = sb("top_f", [P, NT, 8])
    chosen = sb("chosen", [P, 2, NT, E])
    score = sb("score", [P, NT, E])
    combine = sb("combine", [P, NT, E])
    picked = [sb(f"picked{s}", [P, NT]) for s in range(2)]
    small = sb("small", [P, 8, NT])
    stats = sb("stats", [P, NT, 6])
    mean_var = sb("mean_var", [P, NT, 2])
    raw_ug = [sb(f"raw_ug{s}", [P, 2, MC, F]) for s in range(2)]
    raw_d = [sb(f"raw_d{s}", [P, M]) for s in range(2)]
    w_ug = [[sb(f"w_ug{n}{s}", [P, 2, MC, F], F32R) for s in range(2)] for n in range(2)]
    w_d = [[sb(f"w_d{n}{s}", [P, M], F32R) for s in range(2)] for n in range(2)]
    silu = [sb(f"silu{s}", [P, W]) for s in range(2)]
    gated = [sb(f"gated{s}", [P, W]) for s in range(2)]
    hidden = [[sb(f"hidden{n}{s}", [P, W], F32R) for s in range(2)] for n in range(2)]
    yT = sb("yT", [P, MC, T])

    def ps(name):
        return ctx.enter_context(nc.psum_tensor(name, [P, W], F32))

    Y_ps = [[ps(f"Y{m}{w}") for w in range(NW)] for m in range(MC)]
    U_ps, G_ps, B_ps = [ps("U0"), ps("U1")], ps("G"), ps("B")
    banks = [U_ps[0], U_ps[1], G_ps, B_ps]

    x_in, router_in = [sem(f"x1_in{t}") for t in range(NT)], sem("router_in")
    ug_in = [sem("ug_in0"), sem("ug_in1")]
    ident_zero, ident_ready, iota_ready = sem("ident_zero"), sem("ident_ready"), sem("iota_ready")
    r_turned = sem("r_turned")
    dve_step = sem("dve_step")
    var_ready = sem("var_ready")
    dev_ready = sem("dev_ready")
    x1_ready = sem("x1_ready")
    x1_turned = sem("x1_turned")
    x1T_hi, x1T_lo = sem("x1T_hi"), sem("x1T_lo")
    rw_turned, rw_ready = sem("rw_turned"), sem("rw_ready")
    logits_full = sem("logits_full")
    shifted, exp_ready = sem("shifted"), sem("exp_ready")
    combine_ready = sem("combine_ready")
    picked_ready = sem("picked_ready")
    weights_hi = sem("weights_hi")
    parted = sem("parted")
    up_full = sem("up_full")
    gate_full = sem("gate_full")
    down_full = sem("down_full")
    silu_ready = sem("silu_ready")
    product_ready = sem("product_ready")
    gated_ready = sem("gated_ready")
    hid_hi, hid_lo = sem("hid_hi"), sem("hid_lo")
    y_copied, y_turned, y_ready = sem("y_copied"), sem("y_turned"), sem("y_ready")
    out_done = sem("out_done")
    block = ctx.enter_context(nc.Block())

    @block.sync
    def _(sp):
        for t in range(NT):
            sp.dma_start(x1[:, t], x[0, t * P:(t + 1) * P, :]).then_inc(x_in[t], 16)
        sp.dma_start(rw[:], router_w).then_inc(router_in, 16)
        sp.dma_start(bias[:], router_b.rearrange("(o e) -> o e", o=1).to_broadcast([P, E])
                     ).then_inc(router_in, 16)

        def load(e, slot):
            if isinstance(e, int) and e >= E:
                cols = slice((e - E) * F, (e - E + 1) * F)
                up, gate, down = su[0:1, :, cols], sg[0:1, :, cols], sd[0:1, cols, :]
            else:
                up, gate, down = (w[bass.ds(e, 1)] for w in (wu, wg, wd))
            for n, w in ((0, up), (1, gate)):
                sp.dma_start(raw_ug[slot][:, n], w.rearrange("o (c p) f -> p (o c) f", p=P)
                             ).then_inc(ug_in[slot], 16)
            sp.dma_start(raw_d[slot][:], down.rearrange("o f m -> (o f) m")).then_inc(ug_in[slot], 16)

        def unit(it, n):
            e = 2 * it + n // 2
            if n % 2 == 1 and not (isinstance(e, int) and e + 2 >= NE):
                sp.wait_ge(parted, e + 1)
                load(e + 2, (n // 2) % 2)

        load(0, 0)
        load(1, 1)
        unit_walk(sp, unit)
        for t in range(NT):
            sp.wait_ge(y_ready, t + 1)
            sp.dma_start(out[0, t * P:(t + 1) * P, :], y[:, t]).then_inc(out_done, 16)
        sp.wait_ge(out_done, 16 * NT)

    @block.gpsimd
    def _(pool):
        nc.gpsimd.memset(ident[:], 0.0).then_inc(ident_zero, 1)
        pool.wait_ge(ident_zero, 1)
        nc.gpsimd.affine_select(out=ident[:], in_=ident[:], compare_op=ALU.not_equal, fill=1.0, base=0,
                                pattern=[[-1, P]], channel_multiplier=1).then_inc(ident_ready, 1)
        nc.gpsimd.iota(iota_i[:], pattern=[[1, E]], base=0, channel_multiplier=0).then_inc(iota_ready, 1)

        def low(e, slot):
            pool.wait_ge(weights_hi, e + 1)
            nc.gpsimd.tensor_tensor(w_ug[1][slot][:], raw_ug[slot][:], w_ug[0][slot][:].bitcast(F32),
                                    ALU.subtract)
            nc.gpsimd.tensor_tensor(w_d[1][slot][:], raw_d[slot][:], w_d[0][slot][:].bitcast(F32),
                                    ALU.subtract).then_inc(parted, 1)

        def unit(it, n):
            u, e = 4 * it + n, 2 * it + n // 2
            if n % 2 == 1 and not (isinstance(e, int) and e + 1 >= NE):
                low(e + 1, (n // 2 + 1) % 2)
            pool.wait_ge(hid_hi, u + 1)
            nc.gpsimd.tensor_tensor(hidden[1][n % 2][:], gated[n % 2][:], hidden[0][n % 2][:].bitcast(F32),
                                    ALU.subtract).then_inc(hid_lo, 1)

        low(0, 0)
        unit_walk(pool, unit)

    @block.scalar
    def _(act):
        act.wait_ge(var_ready, 1)
        nc.scalar.activation(small[:, 1], small[:, 0], ACT.Sqrt).then_inc(dev_ready, 1)
        for n in range(MC * NW):
            w, c = n // MC, n % MC
            act.wait_ge(x1_turned, n + 1)
            nc.scalar.activation(xT[0][:, c, w * W:(w + 1) * W], Y_ps[c][w][:], ACT.Copy).then_inc(x1T_hi, 1)
        act.wait_ge(shifted, 1)
        nc.scalar.activation(score[:], score[:], ACT.Exp).then_inc(exp_ready, 1)

        def unit(it, n):
            u = 4 * it + n
            act.wait_ge(up_full, u + 1)
            need(act, gated_ready, u - 1)
            nc.scalar.activation(silu[n % 2][:], U_ps[n % 2][:], ACT.Silu).then_inc(silu_ready, 1)
            act.wait_ge(gated_ready, u + 1)
            need(act, down_full, u - 1)
            nc.scalar.activation(hidden[0][n % 2][:], gated[n % 2][:], ACT.Copy).then_inc(hid_hi, 1)

        unit_walk(act, unit)
        act.wait_ge(down_full, UNITS)
        for w in range(NW):
            for m in range(MC):
                nc.scalar.activation(yT[:, m, w * W:(w + 1) * W], Y_ps[m][w][:], ACT.Copy).then_inc(y_copied, 1)
        act.wait_ge(var_ready, 2)
        nc.scalar.activation(small[:, 1], small[:, 0], ACT.Sqrt).then_inc(dev_ready, 1)

    @block.vector
    def _(dve):
        steps = [0]

        def ordered(ins):
            steps[0] += 1
            ins.then_inc(dve_step, 1)
            dve.wait_ge(dve_step, steps[0])

        def add_and_norm(src, dst, turned, ready, which):
            for b in range(NT // 2):
                dve.wait_ge(turned, b + 1)
                if which == 1:
                    dve.wait_ge(x_in[2 * b], 16)
                    dve.wait_ge(x_in[2 * b + 1], 16)
                both = slice(2 * b, 2 * b + 2)
                ordered(nc.vector.tensor_tensor(dst[:, both].rearrange("p t m -> p (t m)"), banks[b][:],
                                                src[:, both].rearrange("p t m -> p (t m)"), ALU.add))
                for t in range(2 * b, 2 * b + 2):
                    ins = nc.vector.bn_stats(stats[:, t], dst[:, t])
                ordered(ins)
            for t in range(NT):
                ins = nc.vector.bn_aggr(mean_var[:, t], stats[:, t])
            ordered(ins)
            nc.vector.tensor_scalar(small[:, 0], mean_var[:, :, 1], EPS, None, ALU.add).then_inc(var_ready, 1)
            dve.wait_ge(dev_ready, which)
            ordered(nc.vector.reciprocal(small[:, 2], small[:, 1]))
            ordered(nc.vector.tensor_tensor(small[:, 3], small[:, 2], small[:, 0], ALU.mult))
            ordered(nc.vector.tensor_tensor(small[:, 4], small[:, 3], small[:, 1], ALU.add))
            ordered(nc.vector.tensor_scalar(small[:, 5], small[:, 4], 0.5, None, ALU.mult))
            ordered(nc.vector.reciprocal(small[:, 6], small[:, 5]))
            for t in range(NT):
                nc.vector.tensor_scalar(dst[:, t], dst[:, t], mean_var[:, t, 0:1], small[:, 6, t:t + 1],
                                        ALU.subtract, ALU.mult).then_inc(ready, 1)

        def high(turn, slot):
            dve.wait_ge(ug_in[slot], 48 * (turn + 1))
            nc.vector.tensor_copy(w_ug[0][slot][:], raw_ug[slot][:])
            nc.vector.tensor_copy(w_d[0][slot][:], raw_d[slot][:]).then_inc(weights_hi, 1)

        add_and_norm(x1, x1, r_turned, x1_ready, 1)
        high(0, 0)
        for n in range(MC * NW):
            w, c = n // MC, n % MC
            cols = slice(w * W, (w + 1) * W)
            dve.wait_ge(x1T_hi, n + 1)
            nc.vector.tensor_tensor(xT[1][:, c, cols], Y_ps[c][w][:], xT[0][:, c, cols].bitcast(F32),
                                    ALU.subtract).then_inc(x1T_lo, 1)
        dve.wait_ge(rw_turned, 1)
        turned = banks[0][:, 0:MC * E].rearrange("p (c e) -> p c e", c=MC)
        ordered(nc.vector.tensor_copy(rwT[0][:], turned))
        nc.vector.tensor_tensor(rwT[1][:], turned, rwT[0][:].bitcast(F32), ALU.subtract).then_inc(rw_ready, 1)
        per_token = lambda a: a.unsqueeze(2).to_broadcast([P, NT, E])
        per_expert = lambda a: a.unsqueeze(1).to_broadcast([P, NT, E])
        dve.wait_ge(logits_full, 1)
        dve.wait_ge(router_in, 32)
        dve.wait_ge(iota_ready, 1)
        got = banks[1][:, 0:NT * E].rearrange("p (t e) -> p t e", t=NT)
        nc.vector.tensor_copy(iota[:], iota_i[:])
        nc.vector.tensor_copy(logits[:], got)
        ordered(nc.vector.tensor_tensor(biased[:], got, per_expert(bias[:]), ALU.add))
        nc.vector.tensor_reduce(small[:, 0], logits[:], AX.X, ALU.max)
        for t in range(NT):
            ins = nc.vector.max(top[:, t], biased[:, t])
        ordered(ins)
        nc.vector.tensor_tensor(score[:], logits[:], per_token(small[:, 0]), ALU.subtract).then_inc(shifted, 1)
        for t in range(NT):
            ins = nc.vector.max_index(top_i[:, t], top[:, t], biased[:, t])
        ordered(ins)
        ordered(nc.vector.tensor_copy(top_f[:], top_i[:]))
        for k in range(2):
            ins = nc.vector.tensor_tensor(chosen[:, k], per_expert(iota[:]), per_token(top_f[:, :, k]),
                                          ALU.is_equal)
        ordered(ins)
        ordered(nc.vector.tensor_tensor(chosen[:, 0], chosen[:, 0], chosen[:, 1], ALU.add))
        dve.wait_ge(exp_ready, 1)
        ordered(nc.vector.tensor_reduce(small[:, 1], score[:], AX.X, ALU.add))
        ordered(nc.vector.reciprocal(small[:, 2], small[:, 1]))
        ordered(nc.vector.tensor_tensor(score[:], score[:], per_token(small[:, 2]), ALU.mult))
        ordered(nc.vector.tensor_tensor(score[:], score[:], chosen[:, 0], ALU.mult))
        ordered(nc.vector.tensor_reduce(small[:, 3], score[:], AX.X, ALU.add))
        ordered(nc.vector.reciprocal(small[:, 4], small[:, 3]))
        nc.vector.tensor_tensor(combine[:], score[:], per_token(small[:, 4]), ALU.mult).then_inc(combine_ready, 1)

        def pick(e, slot):
            nc.vector.tensor_copy(picked[slot][:], combine[:, :, bass.ds(e, 1)].rearrange("p t o -> p (t o)")
                                  ).then_inc(picked_ready, 1)

        dve.wait_ge(combine_ready, 1)
        pick(0, 0)

        def unit(it, n):
            u, e, s = 4 * it + n, 2 * it + n // 2, n % 2
            if s == 1 and not (isinstance(e, int) and e + 1 >= NE):
                need(dve, down_full, u - 1)
                high(it + (n // 2 + 1) // 2, (n // 2 + 1) % 2)
            shared = isinstance(u, int) and u >= E * NW
            dve.wait_ge(silu_ready, u + 1)
            dve.wait_ge(gate_full, u + 1)
            need(dve, hid_lo, u - 1)
            dst = gated[s] if shared else silu[s]
            ins = nc.vector.tensor_tensor(dst[:], G_ps[:], silu[s][:], ALU.mult)
            if not shared:
                ins.then_inc(product_ready, 1)
                dve.wait_ge(product_ready, u + 1)
                ins = nc.vector.tensor_tensor(gated[s][:], B_ps[:], silu[s][:], ALU.mult)
            ins.then_inc(gated_ready, 1)
            if s == 0 and not (isinstance(e, int) and e + 1 >= E):
                pick(e + 1, (n // 2 + 1) % 2)

        unit_walk(dve, unit)
        add_and_norm(x1, y, y_turned, y_ready, 2)

    @block.tensor
    def _(pe):
        pe.wait_ge(ident_ready, 1)

        def turn_back(src, turned, copied):
            for b in range(NT // 2):
                if copied:
                    pe.wait_ge(y_copied, MC * (b // 2 + 1))
                for t in range(2 * b, 2 * b + 2):
                    for c in range(MC):
                        ins = pe.transpose(banks[b][:, (t % 2) * M + c * P:(t % 2) * M + (c + 1) * P],
                                           src[:, c, t * P:(t + 1) * P], ident[:])
                ins.then_inc(turned, 1)

        turn_back(r_acc, r_turned, False)
        for w in range(NW):
            pe.wait_ge(x1_ready, GT * (w + 1))
            for c in range(MC):
                for a in range(GT):
                    ins = pe.transpose(Y_ps[c][w][:, a * P:(a + 1) * P],
                                       x1[:, w * GT + a, c * P:(c + 1) * P], ident[:])
                ins.then_inc(x1_turned, 1)
        pe.wait_ge(router_in, 32)
        for c in range(MC):
            ins = pe.transpose(banks[0][:, c * E:(c + 1) * E], rw[:, c * P:(c + 1) * P], ident[0:E, 0:E])
        ins.then_inc(rw_turned, 1)
        pe.wait_ge(x1T_lo, MC * NW)
        pe.wait_ge(rw_ready, 1)
        for t in range(NT):
            for c in range(MC):
                ins = three(pe, banks[1][:, t * E:(t + 1) * E], [xT[a][:, c, t * P:(t + 1) * P] for a in range(2)],
                            [rwT[a][:, c] for a in range(2)], c == 0, c == MC - 1)
        ins.then_inc(logits_full, 1)

        def down(v, n):
            s, e, w = n % 2, n // 2, n % 2
            pe.wait_ge(hid_lo, v + 1)
            first = isinstance(v, int) and v < NW
            last = isinstance(v, int) and v >= UNITS - NW
            for m in range(MC):
                ins = three(pe, Y_ps[m][w][:], [w_d[a][e % 2][:, m * P:(m + 1) * P] for a in range(2)],
                            [hidden[a][s][:] for a in range(2)], first, last)
            ins.then_inc(down_full, 1)

        def unit(it, n):
            u, e, slot, w = 4 * it + n, 2 * it + n // 2, (n // 2) % 2, n % 2
            shared = isinstance(u, int) and u >= E * NW
            pe.wait_ge(parted, e + 1)
            if isinstance(u, int) and u == 1:
                pe.wait_ge(combine_ready, 1)
            need(pe, silu_ready, u - 1)
            for g, bank in ((0, U_ps[n % 2]), (1, G_ps)):
                if g == 1:
                    need(pe, gated_ready, u)
                for c in range(MC):
                    ins = three(pe, bank[:], [w_ug[a][slot][:, g, c] for a in range(2)],
                                [xT[a][:, c, w * W:(w + 1) * W] for a in range(2)], c == 0, c == MC - 1)
                if g == 0:
                    ins.then_inc(up_full, 1)
            if not shared:
                pe.wait_ge(picked_ready, e + 1)
                for a in range(GT):
                    col = picked[slot][:, w * GT + a:w * GT + a + 1]
                    ins = pe.transpose(B_ps[:, a * P:(a + 1) * P], col.to_broadcast([P, P]), ident[:])
            ins.then_inc(gate_full, 1)
            if not (isinstance(u, int) and u == 0):
                down(u - 1, n - 1 if n else 0)

        unit_walk(pe, unit)
        down(UNITS - 1, UNITS - 1 - 24)
        turn_back(yT, y_turned, True)


_INS = ['L0_attn_x', 'L0_attn_w_aq', 'L0_attn_w_ak', 'L0_attn_w_av', 'L0_attn_w_ao', 'L0_ffn_router_w',
        'L0_ffn_router_bias', 'L0_ffn_Wu', 'L0_ffn_Wg', 'L0_ffn_Wd', 'L0_ffn_Su', 'L0_ffn_Sg', 'L0_ffn_Sd']


def layer(nc, x, wq, wk, wv, wo, router_w, router_b, wu, wg, wd, su, sg, sd, cos_t, sin_t, out):
    with nc.sbuf_tensor("r_acc", [P, MC, T], F32) as r_acc:
        with ExitStack() as ctx:
            attention(nc, ctx, x, wq, wk, wv, wo, cos_t, sin_t, r_acc)
        with ExitStack() as ctx:
            experts(nc, ctx, x, router_w, router_b, wu, wg, wd, su, sg, sd, r_acc, out)


def rotary_tables():
    freqs = np.power(float(ROTARY_BASE), -np.arange(D // 2) / (D // 2)).astype(np.float32)
    angles = (np.arange(T, dtype=np.float32)[None, :] * freqs[:, None]).astype(np.float32)
    cos, sin = np.cos(angles.astype(np.float64)), np.sin(angles.astype(np.float64))
    return (np.concatenate([cos, cos]).astype(np.float32), np.concatenate([-sin, sin]).astype(np.float32))


def kernel(**inputs):
    import concourse.bacc as _bacc
    from concourse.bass_utils import run_bass_kernel_spmd as _run

    nc = _bacc.Bacc("TRN2", target_bir_lowering=False, num_devices=1)
    arrays, args = {}, []
    for name in _INS:
        arrays[name] = np.ascontiguousarray(inputs[name])
    arrays["cos_t"], arrays["sin_t"] = rotary_tables()
    for name, a in arrays.items():
        args.append(nc.dram_tensor(name, a.shape, mybir.dt.from_np(a.dtype), kind="ExternalInput").ap())
    args.append(nc.dram_tensor("out", (1, T, M), F32, kind="ExternalOutput").ap())
    layer(nc, *args)
    return _run(nc, [arrays], core_ids=[0]).results[0]["out"]
```

```python
from contextlib import ExitStack

import numpy as np

import concourse.bass as bass
from concourse import mybir

F32 = mybir.dt.float32
F32R = mybir.dt.float32r
BF16 = mybir.dt.bfloat16
U32 = mybir.dt.uint32
I32 = mybir.dt.int32
ALU = mybir.AluOpType
ACT = mybir.ActivationFunctionType
AX = mybir.AxisListType

P = 128
T, M = 1024, 256
H, D = 16, 128
E, F = 16, 128
NS = 2
MC = M // P
NT = T // P
W = 512
NW = T // W
GT = W // P
NE = E + NS
RAW = 2 * MC * F + M
NTILE = 2 * T // P + E - 1
NWORD = (NTILE + 3 + 3) // 4
NPACK = 4 * NWORD + 4
LOW_POOL = 9
EPS = 1e-5
MASKED = -1e30
ROTARY_BASE = 1250

TURNS = {0: [(0, 0, 0), (1, 1, 1)], 1: [(2, 2, 0), (3, 3, 1)], 2: [(5, 4, 0)], 3: [(6, 5, 0)],
         4: [(7, 6, 0)], 5: [(8, 7, 0)], 6: [(10, 8, 0), (11, 9, 1)], 7: [(12, 10, 0), (13, 11, 1)]}
SPREAD = {2: 4, 6: 9}
TURN_OF = {k: j for turns in TURNS.values() for k, j, _ in turns}
NEVENT, NTURN = 14, 12
LATE = 5


def place_of(i):
    return E + i if i < NS else i - NS


def need(eng, sem, count):
    if not isinstance(count, int) or count > 0:
        eng.wait_ge(sem, count)


def three(eng, out, a, b, start, stop):
    eng.matmul(out, a[0], b[0], start=start, stop=False)
    eng.matmul(out, a[0], b[1], start=False, stop=False)
    return eng.matmul(out, a[1], b[0], start=False, stop=stop)


def event_no(f, k):
    if isinstance(f, int) and f <= 0:
        return max(0, k + 1 - LATE) if f == 0 else 0
    return NEVENT * f + k + 1 - LATE


def turn_no(f, j):
    if isinstance(f, int) and f <= 0:
        return max(0, j - 3) if f == 0 else 0
    return NTURN * f + j - 3


def valued_at(f, i):
    return 0 if i == 6 and f < H else 1 if i == 2 and f > 0 else None


def turned_at(f, i):
    return (f, i) not in ((0, 0), (0, 1), (H, 2))


def rotation_no(f, i):
    return 4 * f + 5 + i // 2


def attend_walk(eng, step):
    for i in range(NT):
        step(0, 0, 0, i)
    with eng.Fori(0, 3) as it:
        for s in range(NT, 5 * NT):
            step(4 * it + s // NT, 2 * it + s // NT // 2, s // NT, s % NT)
    for s in range(13 * NT, H * NT):
        step(s // NT, s // NT // 2, s // NT, s % NT)
    for i in range(3):
        step(H, H // 2, H, i)


def rotated_at(f, fs, i):
    at = f if isinstance(f, int) else 1
    if i % 2 or i == 0 and at == 0 or at >= H or at == H - 1 and i > 0:
        return None
    if i == 0:
        return "k1", fs % 2, rotation_no(f - 1, 6)
    return ["q0", "k0", "q1"][i // 2 - 1], (fs + 1) % 2, rotation_no(f, i - 2)


def chunk_at(f, p, fs, i):
    at = f if isinstance(f, int) else 1
    if at >= H - 1 or at == 0 and i % 2:
        return None
    kind = (["q0", "o00", "k0", "o10", "q1", "o01", "k1", "o11"] if fs % 2 == 0 else
            ["q0", "v0", "k0", "v1", "q1", "v2", "k1", "v3"])[i]
    number = 9 + i // 2 if at == 0 and isinstance(f, int) else 8 * f + 5 + i
    return kind, number, (4 * f + 1 + i // 2 if i % 2 else rotation_no(f, i)), 4 * p + 5 + i // 2


def attention(nc, ctx, x, wq, wk, wv, wo, cos_t, sin_t, rows_in, x_place, r_acc):
    def sb(name, shape, dt=F32):
        return ctx.enter_context(nc.sbuf_tensor(name, shape, dt))

    def sem(name):
        return ctx.enter_context(nc.semaphore(name))

    xT = [sb("xT_hi", [P, MC, T], F32R), sb("xT_lo", [P, MC, T], F32R)]
    cos, sin = x_place[:, 0:T], x_place[:, T:2 * T]
    ident = sb("ident_a", [P, P])
    ident_b = sb("ident_b", [P, P], BF16)
    mask = sb("mask", [P, P], BF16)
    raw_qk = [sb(f"raw_qk{s}", [P, 2, MC, D]) for s in range(2)]
    raw_v = sb("raw_v", [P, MC, 2, D])
    raw_o = sb("raw_o", [P, 2, M])
    w_qk = [[sb(f"w_qk{n}{s}", [P, 2, MC, D], F32R) for s in range(2)] for n in range(2)]
    w_v = [sb(f"w_v{n}", [P, MC, 2, D], F32R) for n in range(2)]
    w_o = [sb(f"w_o{n}", [P, 2, M], F32R) for n in range(2)]
    flat = [sb(f"flat{s}", [P, W]) for s in range(2)]
    swapped = [sb(f"swapped{s}", [P, W]) for s in range(2)]
    rotated = [sb(f"rotated{s}", [P, W]) for s in range(2)]
    QT = [[sb(f"QT{n}{s}", [P, T], F32R) for s in range(2)] for n in range(2)]
    KT = [[sb(f"KT{n}{s}", [P, T], F32R) for s in range(2)] for n in range(2)]
    V = [[sb(f"V{n}{s}", [P, NT, 2 * D], F32R) for s in range(2)] for n in range(2)]
    probs = sb("probs", [P, 4, T])
    PT_full = [sb(f"PT_full{n}", [P, GT, W], F32R) for n in range(2)]
    PT_diag = [sb(f"PT_diag{n}", [P, GT, W], F32R) for n in range(2)]
    spread = sb("spread", [P, W])
    o_buf = sb("o_buf", [P, W])
    OT = [[sb(f"OT{n}{s}", [P, T], F32R) for s in range(2)] for n in range(2)]
    zero_row = sb("zero_row", [P, M])
    spare = sb("spare", [P, NTILE], I32)
    neg_max = sb("neg_max", [P, NT])
    row_sum = sb("row_sum", [P, NT])
    recip = sb("recip", [P, NT])
    x_tok = probs[:, 0:2].rearrange("p s (t m) -> p (s t) m", m=M)

    S_ps = [ctx.enter_context(nc.psum_tensor(f"S{s}", [P, T], F32)) for s in range(2)]
    turn_ps = [ctx.enter_context(nc.psum_tensor(f"turn{s}", [P, W], F32)) for s in range(2)]
    O_ps = ctx.enter_context(nc.psum_tensor("O", [P, W], F32))
    C_ps = ctx.enter_context(nc.psum_tensor("C", [P, W], F32))

    x_in = [sem(f"x_in{h}") for h in range(2)]
    tables_in = sem("tables_in")
    qk_in = [sem("qk_in0"), sem("qk_in1")]
    v_in, o_in = sem("v_in"), sem("o_in")
    zeroed, consts, spared = sem("zeroed"), sem("consts"), sem("spared")
    rows_zeroed, x_back = sem("rows_zeroed"), sem("x_back")
    xT_full, xT_hi, xT_lo = sem("xT_full"), sem("xT_hi"), sem("xT_lo")
    qk_split, v_split, o_split = sem("qk_split"), sem("v_split"), sem("o_split")
    scores_full = sem("scores_full")
    chunk_full = sem("chunk_full")
    turn_full = sem("turn_full")
    values_full = sem("values_full")
    max_ready = sem("max_ready")
    probs_ready = sem("probs_ready")
    turn_hi = sem("turn_hi")
    turn_lo = sem("turn_lo")
    flat_ready = sem("flat_ready")
    swap_in = [sem("swap_in0"), sem("swap_in1")]
    values_hi = sem("values_hi")
    other_read = sem("other_read")
    cos_done = sem("cos_done")
    recip_ready = sem("recip_ready")
    o_scaled = sem("o_scaled")
    o_hi = sem("o_hi")
    o_parted = sem("o_parted")
    sin_done = sem("sin_done")
    rope_sum = sem("rope_sum")
    rope_hi = sem("rope_hi")
    roped = sem("roped")
    qk_hi, v_hi, o_w_hi = sem("qk_hi"), sem("v_hi"), sem("o_w_hi")

    def chunk_bank(i):
        return {0: S_ps[0][:, W:T], 1: S_ps[1][:, W:T], 3: S_ps[1][:, W:T], 5: O_ps[:]}.get(i, C_ps[:])

    def turned_place(n, tile, part):
        g, count = tile // GT, min(GT, tile + 1 - GT * part)
        buf = PT_full[n] if g > part else PT_diag[n]
        return buf[:, 0:count, (tile % GT) * P:(tile % GT + 1) * P], count

    first_banks = [C_ps[:], S_ps[0][:, 0:W], S_ps[0][:, W:T], S_ps[1][:, 0:W], S_ps[1][:, W:T], O_ps[:],
                   turn_ps[0][:], turn_ps[1][:]]
    first_kinds = ["q0", "k0", "q1", "k1", "v0", "v1", "v2", "v3"]

    block = ctx.enter_context(nc.Block())

    @block.sync
    def _(sp):
        for h in range(2):
            sp.dma_start(x_tok[:, h * GT:(h + 1) * GT], x[0, h * W:(h + 1) * W, :].rearrange(
                "(t p) m -> p t m", p=P)).then_inc(x_in[h], 16)
        sp.dma_start(raw_qk[0][:, 0], wq[0].rearrange("(c p) d -> p c d", p=P)).then_inc(qk_in[0], 16)
        sp.dma_start(raw_qk[0][:, 1], wk[0].rearrange("(c p) d -> p c d", p=P)).then_inc(qk_in[0], 16)
        sp.dma_start(cos, cos_t).then_inc(tables_in, 16)
        sp.dma_start(sin, sin_t).then_inc(tables_in, 16)

        def load_qk(h, slot):
            for n, w in ((0, wq), (1, wk)):
                sp.dma_start(raw_qk[slot][:, n], w[bass.ds(h, 1)].rearrange("o (c p) d -> p (o c) d", p=P)
                             ).then_inc(qk_in[slot], 16)

        def load_v(pair):
            for n in range(2):
                sp.dma_start(raw_v[:, :, n], wv[bass.ds(2 * pair + n, 1)].rearrange(
                    "o (c p) d -> p (o c) d", p=P)).then_inc(v_in, 16)

        def load_o(pair):
            sp.dma_start(raw_o[:], wo[bass.ds(2 * pair, 2)].rearrange("n d m -> d n m")).then_inc(o_in, 16)

        def swap(slot, number):
            sp.wait_ge(flat_ready, number)
            for a in range(2):
                sp.dma_start(swapped[slot][(1 - a) * D // 2:(2 - a) * D // 2],
                             flat[slot][a * D // 2:(a + 1) * D // 2]).then_inc(swap_in[slot], 16)

        load_v(0)
        load_qk(1, 1)
        load_o(0)
        for n in range(4):
            swap(n % 2, n + 1)
        sp.wait_ge(qk_split, 1)
        load_qk(2, 0)
        sp.wait_ge(v_split, 1)
        load_v(1)

        def step(f, p, fs, i):
            at = f if isinstance(f, int) else 1
            if i % 2 == 0 and at + 1 < H:
                swap(i // 2 % 2, rotation_no(f, i))
            if i == 7 and at + 3 < H:
                sp.wait_ge(qk_split, f + 2)
                load_qk(f + 3, (fs + 3) % 2)
            if i == 3 and at < H:
                count = 2 if at < H - 1 else NTILE - 2 * (H - 1)
                sp.dma_start(rows_in.rearrange("(j p) m -> p j m", p=P)[:, bass.ds(2 * f, count), 0:M],
                             zero_row[:].unsqueeze(1).to_broadcast([P, count, M])).then_inc(rows_zeroed, 16)
            if i == 7 and fs % 2 == 1:
                if at // 2 + 2 < H // 2:
                    sp.wait_ge(v_split, p + 2)
                    load_v(p + 2)
                if at // 2 + 1 < H // 2:
                    sp.wait_ge(o_split, p + 1)
                    load_o(p + 1)

        sp.wait_ge(spared, 2)
        attend_walk(sp, step)
        sp.wait_ge(rope_sum, 4 * H)
        x_tiles = x_place[:].rearrange("p (t m) -> p t m", t=NT)[:, :, 0:M]
        for b in range(NT // 2):
            sp.dma_start(x_tiles[:, 2 * b:2 * b + 2], x[0, 2 * b * P:(2 * b + 2) * P, :].rearrange(
                "(t p) m -> p t m", p=P)).then_inc(x_back, 16)
        sp.dma_start(rows_in[:, M:M + 1].rearrange("(j p) o -> p (j o)", p=P).bitcast(I32), spare[:],
                     allow_slow_non_contiguous=True
                     ).then_inc(rows_zeroed, 16)
        sp.wait_ge(rows_zeroed, 16 * (H + 1))
        sp.wait_ge(x_back, 16 * NT // 2)

    @block.gpsimd
    def _(pool):
        nc.gpsimd.memset(ident[:], 0.0).then_inc(zeroed, 1)
        nc.gpsimd.memset(ident_b[:], 0.0).then_inc(zeroed, 1)
        nc.gpsimd.memset(mask[:], 0.0).then_inc(zeroed, 1)
        pool.wait_ge(zeroed, 3)
        for m in (ident, ident_b):
            nc.gpsimd.affine_select(out=m[:], in_=m[:], compare_op=ALU.not_equal, fill=1.0, base=0,
                                    pattern=[[-1, P]], channel_multiplier=1).then_inc(consts, 1)
        nc.gpsimd.affine_select(out=mask[:], in_=mask[:], compare_op=ALU.is_ge, fill=MASKED, base=0,
                                pattern=[[-1, P]], channel_multiplier=1).then_inc(consts, 1)

        nc.gpsimd.memset(zero_row[:], 0.0).then_inc(spared, 1)
        nc.gpsimd.iota(spare[:], pattern=[[P, NTILE]], base=2 * T, channel_multiplier=1).then_inc(spared, 1)

        nc.gpsimd.memset(r_acc[:], 0.0).then_inc(zeroed, 1)

        def low(raw, hi, lo, hi_sem, count, ready):
            pool.wait_ge(hi_sem, count)
            nc.gpsimd.tensor_tensor(lo, raw, hi.bitcast(F32), ALU.subtract).then_inc(ready, 1)

        def low_qk(h, slot):
            low(raw_qk[slot][:], w_qk[0][slot][:], w_qk[1][slot][:], qk_hi, h + 1, qk_split)

        def low_v(pair):
            low(raw_v[:], w_v[0][:], w_v[1][:], v_hi, pair + 1, v_split)

        def low_o(pair):
            low(raw_o[:], w_o[0][:], w_o[1][:], o_w_hi, pair + 1, o_split)

        def rotate(kind, number, use):
            slot, half = "qk".index(kind[0]), int(kind[1])
            pool.wait_ge(swap_in[slot], 32 * use)
            nc.gpsimd.tensor_tensor(swapped[slot][:], swapped[slot][:], sin[:, half * W:(half + 1) * W],
                                    ALU.mult).then_inc(sin_done, 1)
            pool.wait_ge(cos_done, number)
            pool.wait_ge(sin_done, number)
            nc.gpsimd.tensor_tensor(rotated[slot][:], rotated[slot][:], swapped[slot][:], ALU.add
                                    ).then_inc(rope_sum, 1)

        def low_rotated(kind, dst, number):
            cols = slice(int(kind[1]) * W, (int(kind[1]) + 1) * W)
            bufs = QT if kind[0] == "q" else KT
            low(rotated["qk".index(kind[0])][:], bufs[0][dst][:, cols], bufs[1][dst][:, cols],
                rope_hi, number, roped)

        def step(f, p, fs, i):
            at = f if isinstance(f, int) else 1
            ch, before = chunk_at(f, p, fs, i), rotated_at(f, fs, i)
            if before:
                low_rotated(*before)
            if ch and i % 2 == 0:
                rotate(ch[0], ch[2], 2 * f + 3 + i // 4)
            if i == 1 and fs % 2 == 0 and at // 2 + 1 < H // 2:
                low_v(p + 1)
            if i == 1 and fs % 2 == 1:
                low_o(p)
            if i == 5 and at + 2 < H:
                low_qk(f + 2, fs % 2)

        low_qk(0, 0)
        low_v(0)
        for n in range(4):
            low_rotated(first_kinds[n], 0, n + 1)
            if n == 1:
                low_qk(1, 1)
        attend_walk(pool, step)

    @block.scalar
    def _(act):
        for n in range(NW * MC):
            w, c = n // MC, n % MC
            act.wait_ge(xT_full, n + 1)
            nc.scalar.activation(xT[0][:, c, w * W:(w + 1) * W], S_ps[c][:, w * W:(w + 1) * W],
                                 ACT.Copy).then_inc(xT_hi, 1)

        def read_chunk(kind, bank, pair_slot, number, nth):
            act.wait_ge(chunk_full, number)
            if kind[0] == "v":
                t = 2 * int(kind[1])
                nc.scalar.activation(V[0][pair_slot][:, t:t + 2].rearrange("p a b -> p (a b)"), bank,
                                     ACT.Copy).then_inc(values_hi, 1)
                return
            slot = "qk".index(kind[0])
            if not isinstance(nth, int) or nth > 2:
                act.wait_ge(rope_sum, nth - 2)
            nc.scalar.activation(flat[slot][:], bank, ACT.Copy, scale=1.0 / D if kind[0] == "q" else 1.0
                                 ).then_inc(flat_ready, 1)

        def high_rotated(kind, dst, number):
            cols = slice(int(kind[1]) * W, (int(kind[1]) + 1) * W)
            act.wait_ge(rope_sum, number)
            nc.scalar.activation((QT if kind[0] == "q" else KT)[0][dst][:, cols],
                                 rotated["qk".index(kind[0])][:], ACT.Copy).then_inc(rope_hi, 1)

        def high_out(f, fs, g):
            act.wait_ge(o_scaled, 2 * f + g + 1)
            nc.scalar.activation(OT[0][fs % 2][:, g * W:(g + 1) * W], o_buf[:], ACT.Copy).then_inc(o_hi, 1)

        def step(f, p, fs, i):
            at = f if isinstance(f, int) else 1
            ch, before = chunk_at(f, p, fs, i), rotated_at(f, fs, i)
            if i == 3 and at > 0:
                high_out(f - 1, fs - 1, 1)
            if i == 7:
                high_out(f, fs, 0)
            if ch and ch[0][0] != "o":
                read_chunk(ch[0], chunk_bank(i), (fs // 2 + 1) % 2, ch[1], ch[2])
            g = valued_at(at, i)
            if g is not None:
                act.wait_ge(turn_full, event_no(f, SPREAD[i]))
                need(act, o_scaled, 2 * f + (0 if g == 0 else -1))
                nc.scalar.activation(spread[:], turn_ps[SPREAD[i] % 2][:], ACT.Copy).then_inc(turn_hi, 1)
            if turned_at(at, i):
                for k, _, part in TURNS[i]:
                    act.wait_ge(turn_full, event_no(f, k))
                    out, n = turned_place(0, (i - 2) % NT, part)
                    nc.scalar.activation(out, turn_ps[k % 2][:, 0:n * P].rearrange("p (a b) -> p a b", a=n),
                                         ACT.Copy).then_inc(turn_hi, 1)
            if at < H:
                act.wait_ge(max_ready, NT * f + i + 1)
                w = (i + 1) * P
                if i == 0:
                    need(act, recip_ready, 2 * f - 1)
                if i == GT:
                    need(act, recip_ready, 2 * f)
                nc.scalar.activation(probs[:, i % 4, 0:w], S_ps[i % 2][:, 0:w], ACT.Exp,
                                     bias=neg_max[:, i:i + 1], accum_out=row_sum[:, i:i + 1]
                                     ).then_inc(probs_ready, 1)
            if before:
                high_rotated(*before)

        for n, kind in enumerate(first_kinds[:4]):
            if n >= 2:
                high_rotated(first_kinds[n - 2], 0, n - 1)
            read_chunk(kind, first_banks[n], 0, n + 1, n + 1)
        for n in range(4, 8):
            read_chunk(first_kinds[n], first_banks[n], 0, n + 1, n + 1)
            if n in (5, 6):
                high_rotated(first_kinds[n - 3], 0, n - 2)
        attend_walk(act, step)
        high_out(H - 1, H - 1, 1)

    @block.vector
    def _(dve):
        def high_first():
            dve.wait_ge(qk_in[0], 32)
            nc.vector.tensor_copy(w_qk[0][0][:], raw_qk[0][:]).then_inc(qk_hi, 1)

        high_first()
        for n in range(NW * MC):
            w, c = n // MC, n % MC
            dve.wait_ge(xT_hi, n + 1)
            nc.vector.tensor_tensor(xT[1][:, c, w * W:(w + 1) * W], S_ps[c][:, w * W:(w + 1) * W],
                                    xT[0][:, c, w * W:(w + 1) * W].bitcast(F32), ALU.subtract
                                    ).then_inc(xT_lo, 1)

        def read_chunk(kind, bank, pair_slot, number, nth, v_no):
            if kind[0] in "qk":
                slot, half = "qk".index(kind[0]), int(kind[1])
                dve.wait_ge(flat_ready, nth)
                need(dve, roped, nth - 2)
                nc.vector.tensor_tensor(rotated[slot][:], flat[slot][:], cos[:, half * W:(half + 1) * W],
                                        ALU.mult).then_inc(cos_done, 1)
            elif kind[0] == "v":
                t = 2 * int(kind[1])
                dve.wait_ge(values_hi, v_no)
                nc.vector.tensor_tensor(V[1][pair_slot][:, t:t + 2].rearrange("p a b -> p (a b)"), bank,
                                        V[0][pair_slot][:, t:t + 2].rearrange("p a b -> p (a b)").bitcast(F32),
                                        ALU.subtract).then_inc(other_read, 1)
            else:
                c, w = int(kind[1]), int(kind[2])
                dve.wait_ge(chunk_full, number)
                nc.vector.tensor_tensor(r_acc[:, c, w * W:(w + 1) * W], bank,
                                        r_acc[:, c, w * W:(w + 1) * W], ALU.add).then_inc(other_read, 1)

        def high_qk(h, turn, slot):
            dve.wait_ge(qk_in[slot], 32 * (turn + 1))
            nc.vector.tensor_copy(w_qk[0][slot][:], raw_qk[slot][:]).then_inc(qk_hi, 1)

        def high_v(pair):
            dve.wait_ge(v_in, 32 * (pair + 1))
            nc.vector.tensor_copy(w_v[0][:], raw_v[:]).then_inc(v_hi, 1)

        def high_o(pair):
            dve.wait_ge(o_in, 16 * (pair + 1))
            nc.vector.tensor_copy(w_o[0][:], raw_o[:]).then_inc(o_w_hi, 1)

        def low_out(f, fs, g):
            cols = slice(g * W, (g + 1) * W)
            dve.wait_ge(o_hi, 2 * f + g + 1)
            nc.vector.tensor_tensor(OT[1][fs % 2][:, cols], o_buf[:], OT[0][fs % 2][:, cols].bitcast(F32),
                                    ALU.subtract).then_inc(o_parted, 1)

        def reciprocals(f, g):
            dve.wait_ge(probs_ready, NT * f + GT * (g + 1))
            nc.vector.reciprocal(recip[:, g * GT:(g + 1) * GT], row_sum[:, g * GT:(g + 1) * GT]
                                 ).then_inc(recip_ready, 1)

        def step(f, p, fs, i):
            at = f if isinstance(f, int) else 1
            if at < H:
                dve.wait_ge(scores_full, NT * f + i + 1)
                nc.vector.tensor_reduce(neg_max[:, i:i + 1], S_ps[i % 2][:, 0:(i + 1) * P], AX.X, ALU.max,
                                        negate=True).then_inc(max_ready, 1)
            if i == 3 and at > 0:
                low_out(f - 1, fs - 1, 1)
            if i == 7:
                low_out(f, fs, 0)
            ch = chunk_at(f, p, fs, i)
            if ch:
                read_chunk(ch[0], chunk_bank(i), (fs // 2 + 1) % 2, *ch[1:])
            if turned_at(at, i):
                for k, j, part in TURNS[i]:
                    dve.wait_ge(turn_hi, event_no(f, k))
                    hi, n = turned_place(0, (i - 2) % NT, part)
                    nc.vector.tensor_tensor(turned_place(1, (i - 2) % NT, part)[0],
                                            turn_ps[k % 2][:, 0:n * P].rearrange("p (a b) -> p a b", a=n),
                                            hi.bitcast(F32), ALU.subtract).then_inc(turn_lo, 1)
            if i == 0 and fs % 2 == 0 and at // 2 + 1 < H // 2:
                dve.wait_ge(chunk_full, 8 if at == 0 else 16 * p + 4)
                high_v(p + 1)
            if i == 0 and fs % 2 == 1:
                dve.wait_ge(chunk_full, 16 * p + 12)
                high_o(p)
            if i == 4 and at + 2 < H:
                high_qk(f + 2, p + 1, fs % 2)
            if i == 1 and at > 0:
                reciprocals(f - 1, 1)
            if i == 5 and at < H:
                reciprocals(f, 0)
            g = valued_at(at, i)
            if g is not None:
                n = 2 * f + 1 - g
                dve.wait_ge(values_full, n)
                dve.wait_ge(turn_hi, event_no(f, SPREAD[i]))
                need(dve, o_parted, n - 1)
                nc.vector.tensor_tensor(o_buf[:], O_ps[:], spread[:], ALU.mult).then_inc(o_scaled, 1)

        high_v(0)
        dve.wait_ge(tables_in, 32)
        for n, kind in enumerate(first_kinds[:4]):
            read_chunk(kind, first_banks[n], 0, n + 1, n + 1, 0)
            for v in {2: [4], 3: [5, 6]}.get(n, []):
                read_chunk(first_kinds[v], first_banks[v], 0, v + 1, v + 1, v - 3)
            slot, half = n % 2, n // 2
            dve.wait_ge(swap_in[slot], 32 * (half + 1))
            nc.vector.tensor_tensor(swapped[slot][:], swapped[slot][:], sin[:, half * W:(half + 1) * W],
                                    ALU.mult).then_inc(sin_done, 1)
            dve.wait_ge(cos_done, n + 1)
            dve.wait_ge(sin_done, n + 1)
            nc.vector.tensor_tensor(rotated[slot][:], rotated[slot][:], swapped[slot][:], ALU.add
                                    ).then_inc(rope_sum, 1)
            if n == 1:
                high_qk(1, 0, 1)
        read_chunk(first_kinds[7], first_banks[7], 0, 8, 8, 4)
        dve.wait_ge(zeroed, 4)
        attend_walk(dve, step)
        low_out(H - 1, H - 1, 1)
        for n in range(4):
            read_chunk(["o00", "o10", "o01", "o11"][n], first_banks[n], 0, 8 * (H - 1) + 5 + n, 0, 0)

    @block.tensor
    def _(pe):
        pe.wait_ge(consts, 3)
        for w in range(NW):
            for c in range(MC):
                for q in range(GT):
                    t = w * GT + q
                    pe.wait_ge(x_in[w], 16)
                    ins = pe.transpose(S_ps[c][:, t * P:(t + 1) * P], x_tok[:, t, c * P:(c + 1) * P], ident[:])
                ins.then_inc(xT_full, 1)
        pe.wait_ge(xT_lo, NW * MC)

        def chunk(kind, bank, head_slot, pair_slot):
            for c in range(2):
                if kind[0] in "qk":
                    n, w = "qk".index(kind[0]), int(kind[1])
                    ins = three(pe, bank, [w_qk[a][head_slot][:, n, c] for a in range(2)],
                                [xT[a][:, c, w * W:(w + 1) * W] for a in range(2)], c == 0, c == 1)
                elif kind[0] == "o":
                    m, w = int(kind[1]), int(kind[2])
                    ins = three(pe, bank, [w_o[a][:, c, m * P:(m + 1) * P] for a in range(2)],
                                [OT[a][c][:, w * W:(w + 1) * W] for a in range(2)], c == 0, c == 1)
            if kind[0] == "v":
                for a in range(2):
                    t = 2 * int(kind[1]) + a
                    for c in range(2):
                        ins = three(pe, bank[:, a * M:(a + 1) * M],
                                    [xT[b][:, c, t * P:(t + 1) * P] for b in range(2)],
                                    [w_v[b][:, c].rearrange("p a b -> p (a b)") for b in range(2)],
                                    c == 0, c == 1)
            ins.then_inc(chunk_full, 1)

        def scores(f, fs, i):
            s, w = fs % 2, (i + 1) * P
            need(pe, roped, 4 * f + (2 if i < GT else 4))
            need(pe, probs_ready, NT * f + i - 1)
            if i == GT and not (isinstance(f, int) and f == H - 1):
                pe.wait_ge(flat_ready, rotation_no(f, 0))
            if i == GT + 1 and not (isinstance(f, int) and f in (0, H - 1)):
                pe.wait_ge(other_read, 4 * f + 2)
            q = [QT[a][s][:, i * P:(i + 1) * P] for a in range(2)]
            spans = [(a, min(a + W, w)) for a in range(0, w, W)]
            for a, b in spans:
                pe.matmul(S_ps[i % 2][:, a:b], q[0], KT[0][s][:, a:b], start=True, stop=False)
                pe.matmul(S_ps[i % 2][:, a:b], q[0], KT[1][s][:, a:b], start=False, stop=False)
            for a, b in spans:
                pe.matmul(S_ps[i % 2][:, a:b], q[1], KT[0][s][:, a:b], start=False, stop=b < w)
            pe.matmul(S_ps[i % 2][:, w - P:w], ident_b[:], mask[:], start=False, stop=True
                      ).then_inc(scores_full, 1)

        def turn_bank_free(f, k):
            f, k = (f, k - 2) if k >= 2 else (f - 1, k - 2 + NEVENT)
            if k in SPREAD.values():
                need(pe, turn_hi, event_no(f, k))
            else:
                need(pe, turn_lo, turn_no(f, TURN_OF[k]))

        def turn(f, fs, tile, k, part):
            turn_bank_free(f, k)
            n = min(GT, tile + 1 - GT * part)
            for a in range(n):
                kt = GT * part + a
                ins = pe.transpose(turn_ps[k % 2][:, a * P:(a + 1) * P],
                                   probs[:, tile % 4, kt * P:(kt + 1) * P], ident[:])
            ins.then_inc(turn_full, 1)

        def step(f, p, fs, i):
            at = f if isinstance(f, int) else 1
            if at < H:
                scores(f, fs, i)
            if i == 2 and isinstance(f, int) and f == 0:
                pe.wait_ge(other_read, 4)
            ch = chunk_at(f, p, fs, i)
            if ch:
                kind, _, nth, _ = ch
                if i == 2 and at:
                    pe.wait_ge(flat_ready, rotation_no(f - 1, 6))
                    pe.wait_ge(other_read, 4 * f)
                if i == 3:
                    pe.wait_ge(other_read, 4 * f + 1)
                if i == 5:
                    pe.wait_ge(o_scaled, 2 * f)
                if i in (4, 6, 7):
                    pe.wait_ge(flat_ready, rotation_no(f, {4: 2, 6: 4, 7: 6}[i]))
                if kind[0] in "qk":
                    pe.wait_ge(qk_split, f + 2)
                elif kind[0] == "v":
                    pe.wait_ge(v_split, p + 2)
                else:
                    pe.wait_ge(o_split, p)
                    pe.wait_ge(o_parted, 2 * f - 1 + int(kind[2]))
                chunk(kind, chunk_bank(i), (fs + 1) % 2, (fs // 2 + 1) % 2)
            g, turning, tile = valued_at(at, i), turned_at(at, i), (i - 2) % NT
            if g is not None:
                k, n = SPREAD[i], 2 * f + 1 - g
                turn_bank_free(f, k)
                pe.wait_ge(recip_ready, n)
                for a in range(GT):
                    col = recip[:, g * GT + a:g * GT + a + 1]
                    ins = pe.transpose(turn_ps[k % 2][:, a * P:(a + 1) * P], col.to_broadcast([P, P]), ident[:])
                ins.then_inc(turn_full, 1)
            if turning:
                pe.wait_ge(probs_ready, NT * f + i - 1)
                if g != 1:
                    turn(f, fs, tile, TURNS[i][0][0], 0)
            if g is not None:
                hs = fs - g
                need(pe, o_scaled, n - 1)
                if g == 0 and at and at < H - 1:
                    pe.wait_ge(other_read, 4 * f + 3)
                pe.wait_ge(turn_lo, turn_no(f, 7 if g == 0 else 3))
                if g == 0 and fs % 2 == 0:
                    pe.wait_ge(other_read, 4 if at == 0 else 8 * p)
                for j in range(GT * (g + 1)):
                    a = max(0, j - GT * g) * P
                    buf = PT_diag if j >= GT * g else PT_full
                    ins = three(pe, O_ps[:, a:W],
                                [V[b][(hs // 2) % 2][:, j, (hs % 2) * D:(hs % 2 + 1) * D] for b in range(2)],
                                [buf[b][:, j % GT, a:W] for b in range(2)], j == 0, j == GT * (g + 1) - 1)
                ins.then_inc(values_full, 1)
            if turning and g == 1:
                turn(f, fs, tile, TURNS[i][0][0], 0)
            if turning and len(TURNS[i]) > 1:
                turn(f, fs, tile, TURNS[i][1][0], 1)

        for n, kind in enumerate(first_kinds):
            if n == 0:
                pe.wait_ge(qk_split, 1)
            if n == 4:
                pe.wait_ge(v_split, 1)
            chunk(kind, first_banks[n], 0, 0)
        pe.wait_ge(flat_ready, 4)
        attend_walk(pe, step)
        pe.wait_ge(probs_ready, NT * H)
        for n in range(4):
            kind = ["o00", "o10", "o01", "o11"][n]
            pe.wait_ge(o_split, H // 2)
            pe.wait_ge(o_parted, 2 * H - 1 + int(kind[2]))
            pe.wait_ge(other_read, 4 * (H - 1))
            chunk(kind, first_banks[n], 0, 0)


def tile_walk(eng, step, start=7):
    for n in range(start):
        step(0, n)
    with eng.Fori(0, 3) as it:
        for n in range(start, start + 8):
            step(it, n)
    for n in range(start, NTILE + 3 - 24):
        step(3, n)


def experts(nc, ctx, router_w, router_b, wu, wg, wd, su, sg, sd, rows_in, rows_out, xa, y, r_acc, out):
    def sb(name, shape, dt=F32):
        return ctx.enter_context(nc.sbuf_tensor(name, shape, dt))

    def sem(name):
        return ctx.enter_context(nc.semaphore(name))

    ident = sb("ident_f", [P, P])
    ones = sb("ones", [P, P], BF16)
    below = sb("below", [P, P], BF16)
    xT = [sb(f"x1T{n}", [P, MC, T], F32R) for n in range(2)]
    yT = sb("yT", [P, MC, T])
    y_rows = [yT[:].rearrange("p c t -> p (c t)").rearrange("p (t m) -> p t m", m=M), xa[1][:, :, 0:M]]
    rw = sb("rw", [E, M])
    rwT = [sb(f"rwT{n}", [P, MC, E], F32R) for n in range(2)]
    bias = sb("bias", [P, E])
    iota_i = sb("iota_i", [P, E], I32)
    tile_i = sb("tile_i", [1, NPACK], I32)
    iota = sb("iota", [P, E])
    tile_f = sb("tile_f", [1, NPACK])
    upto = sb("upto", [P, E, E])
    logits = sb("logits", [P, NT, E])
    biased = sb("biased", [P, NT, E])
    top = sb("top", [P, NT, 8])
    top_i = sb("top_i", [P, NT, 8], U32)
    top_f = sb("top_f", [P, NT, 8])
    chosen = sb("chosen", [P, 2, NT, E])
    picked = sb("picked", [P, 2, NT, E])
    chosen_b = sb("chosen_b", [P, NT + 1, E], BF16)
    score = sb("score", [P, NT, E])
    wide = sb("wide", [P, E, E])
    ends = sb("ends", [P, E])
    tiles = sb("tiles", [P, E])
    place_f = sb("place_f", [P, 2, NT])
    place = sb("place", [P, 2, NT], U32)
    share = sb("share", [P, 2, NT])
    owner_w = sb("owner_w", [1, NPACK, E], BF16)
    owner_f = sb("owner_f", [1, NPACK])
    packed_f = sb("packed_f", [1, NWORD])
    packed = sb("packed", [1, NWORD], I32)
    targets = sb("targets", [P, NTILE], I32)
    small = sb("small", [P, 8, NT])
    stats = sb("stats", [P, NT, 6])
    mean_var = sb("mean_var", [P, NT, 2])
    raw = [sb(f"raw{s}", [P, RAW]) for s in range(4)]
    w_all = [sb(f"w_all{n}", [P, NE, RAW], F32R) for n in range(2)]
    silu = [sb(f"silu{s}", [P, W]) for s in range(2)]
    hidden = [[sb(f"hidden{n}{s}", [P, W], F32R) for s in range(2)] for n in range(2)]
    flat_logits = [silu[w][0:E] for w in range(NW)]
    x_rows = [sb(f"x_rows{s}", [P, M]) for s in range(4)]
    xtT = [[sb(f"xtT{n}{s}", [P, M], F32R) for s in range(2)] for n in range(2)]
    act_t = [sb(f"act_t{s}", [P, F]) for s in range(2)]
    hT = [[sb(f"hT{n}{s}", [P, P], F32R) for s in range(2)] for n in range(2)]
    out_rows = [sb(f"out_rows{s}", [P, M]) for s in range(4)]

    def ps(name):
        return ctx.enter_context(nc.psum_tensor(name, [P, W], F32))

    Y_ps = [[ps(f"Y{m}{w}") for w in range(NW)] for m in range(MC)]
    U_ps, G_ps = [ps("U0"), ps("U1")], [ps("G0"), ps("G1")]
    banks = [U_ps[0], U_ps[1], G_ps[0], G_ps[1]]
    rw_ps, logits_ps, rank_ps = Y_ps[1][1], Y_ps[0][1], Y_ps[1][0]
    flat_ps = G_ps
    TX, UG, HT, DN = Y_ps[0], U_ps, G_ps, Y_ps[1]

    router_in = sem("router_in")
    w_in = [sem(f"w_in{s}") for s in range(4)]
    ident_ready = sem("ident_ready")
    zero_f, consts_f = sem("zero_f"), sem("consts_f")
    r_turned = sem("r_turned")
    dve_step = sem("dve_step")
    var_ready = sem("var_ready")
    dev_ready = sem("dev_ready")
    x1_ready = sem("x1_ready")
    x1_copied = sem("x1_copied")
    x1_turned = sem("x1_turned")
    x1T_hi, x1T_lo = sem("x1T_hi"), sem("x1T_lo")
    rw_turned, rw_ready = sem("rw_turned"), sem("rw_ready")
    flat_full, flat_copied = sem("flat_full"), sem("flat_copied")
    logits_full = sem("logits_full")
    shifted, exp_ready = sem("shifted"), sem("exp_ready")
    chosen_ready = sem("chosen_ready")
    ranks_full = sem("ranks_full")
    place_ready = sem("place_ready")
    owner_ready = sem("owner_ready")
    weights_hi = sem("weights_hi")
    parted = sem("parted")
    parted_dve = sem("parted_dve")
    up_full, gate_full = sem("up_full"), sem("gate_full")
    silu_ready, gated_ready = sem("silu_ready"), sem("gated_ready")
    hid_hi, hid_lo = sem("hid_hi"), sem("hid_lo")
    down_full = sem("down_full")
    y_copied, y_turned = sem("y_copied"), sem("y_turned")
    sum_ready = sem("sum_ready")
    scattered = sem("scattered")
    targets_in = sem("targets_in")
    rows_read = [sem(f"rows_read{s}") for s in range(4)]
    tx_full, tx_hi, tx_lo = sem("tx_full"), sem("tx_hi"), sem("tx_lo")
    ug_full = sem("ug_full")
    act_ready = sem("act_ready")
    prod_ready = sem("prod_ready")
    ht_full, ht_hi, ht_lo = sem("ht_full"), sem("ht_hi"), sem("ht_lo")
    dn_full = sem("dn_full")
    rows_ready = sem("rows_ready")
    rows_out_done = [sem(f"rows_out{s}") for s in range(4)]
    y_in = [[sem(f"y_in{k}_{t}") for t in range(NT)] for k in range(2)]
    share_ready = sem("share_ready")
    first_scaled = sem("first_scaled")
    first_added = sem("first_added")
    tail_ready = sem("tail_ready")
    norm_ready = sem("norm_ready")
    y_ready = sem("y_ready")
    out_done = sem("out_done")
    block = ctx.enter_context(nc.Block())

    @block.sync
    def _(sp):
        sp.dma_start(rw[:], router_w).then_inc(router_in, 16)
        sp.dma_start(bias[:], router_b.rearrange("(o e) -> o e", o=1).to_broadcast([P, E])
                     ).then_inc(router_in, 16)

        def load(up, gate, down, slot):
            ug = raw[slot][:, 0:2 * MC * F].rearrange("p (c n f) -> p c n f", c=MC, n=2)
            for n, w in ((0, up), (1, gate)):
                sp.dma_start(ug[:, :, n], w.rearrange("o (c p) f -> p (o c) f", p=P)).then_inc(w_in[slot], 16)
            sp.dma_start(raw[slot][:, 2 * MC * F:RAW], down.rearrange("o f m -> (o f) m")
                         ).then_inc(w_in[slot], 16)

        def load_expert(e, slot):
            load(wu[bass.ds(e, 1)], wg[bass.ds(e, 1)], wd[bass.ds(e, 1)], slot)

        for i in range(NS):
            cols = slice(i * F, (i + 1) * F)
            load(su[0:1, :, cols], sg[0:1, :, cols], sd[0:1, cols, :], i)
        for e in range(2):
            load_expert(e, NS + e)
        with sp.Fori(0, 2) as it:
            for n in range(4):
                sp.wait_ge(parted, 4 * it + n + 1)
                load_expert(4 * it + n + 2, n)
        for i in range(12, NE):
            sem_of, count = (parted, i - 3) if i - 4 < LOW_POOL else (parted_dve, i - 3 - LOW_POOL)
            sp.wait_ge(sem_of, count)
            load_expert(i - NS, i % 4)

        sp.wait_ge(scattered, 16 * 2 * NT)
        tile_rows = rows_in.rearrange("(j p) m -> j p m", p=P)
        def step(it, n):
            j = 8 * it + n
            if isinstance(j, int) and j >= NTILE:
                return
            need(sp, tx_full, j - 3)
            sp.dma_start(x_rows[n % 4][:], tile_rows[bass.ds(j, 1), :, 0:M].rearrange("o p m -> (o p) m")
                         ).then_inc(rows_read[n % 4], 16)
            if isinstance(j, int) and j == 3:
                sp.dma_start(targets[:], rows_in[:, M:M + 1].rearrange("(j p) o -> p (j o)", p=P).bitcast(I32),
                             allow_slow_non_contiguous=True).then_inc(targets_in, 16)

        tile_walk(sp, step)
        for s in range(4):
            sp.wait_ge(rows_out_done[s], 16 * len(range(s, NTILE, 4)))
        for t in range(NT):
            for k in range(2):
                sp.dma_start(y_rows[k][:, t], rows_out[k * T + t * P:k * T + (t + 1) * P, :]
                             ).then_inc(y_in[k][t], 16)
        for t in range(NT):
            if t < NT - 2:
                sp.wait_ge(y_ready, t + 1)
            else:
                sp.wait_ge(tail_ready, t - NT + 3)
            sp.dma_start(out[0, t * P:(t + 1) * P, :], y[:, t]).then_inc(out_done, 16)
        sp.wait_ge(out_done, 16 * NT)

    @block.gpsimd
    def _(pool):
        nc.gpsimd.memset(ident[:], 0.0).then_inc(zero_f, 1)
        pool.wait_ge(zero_f, 1)
        nc.gpsimd.affine_select(out=ident[:], in_=ident[:], compare_op=ALU.not_equal, fill=1.0, base=0,
                                pattern=[[-1, P]], channel_multiplier=1).then_inc(ident_ready, 1)
        nc.gpsimd.memset(ones[:], 1.0).then_inc(zero_f, 1)
        nc.gpsimd.memset(below[:], 1.0).then_inc(zero_f, 1)
        nc.gpsimd.memset(chosen_b[:], 0.0).then_inc(zero_f, 1)
        nc.gpsimd.memset(upto[:], 1.0).then_inc(zero_f, 1)
        pool.wait_ge(zero_f, 5)
        nc.gpsimd.affine_select(out=below[:], in_=below[:], compare_op=ALU.is_ge, fill=0.0, base=-1,
                                pattern=[[1, P]], channel_multiplier=-1).then_inc(consts_f, 1)
        nc.gpsimd.affine_select(out=upto[:], in_=upto[:], compare_op=ALU.is_ge, fill=0.0, base=0,
                                pattern=[[1, E], [-1, E]], channel_multiplier=0).then_inc(consts_f, 1)
        nc.gpsimd.iota(iota_i[:], pattern=[[1, E]], base=0, channel_multiplier=0).then_inc(consts_f, 1)
        nc.gpsimd.iota(tile_i[:], pattern=[[1, NPACK]], base=-3, channel_multiplier=0).then_inc(consts_f, 1)
        for k in range(2):
            nc.gpsimd.iota(xa[k][:, :, M:M + 1].bitcast(I32), pattern=[[P, NT], [0, 1]], base=k * T,
                           channel_multiplier=1).then_inc(consts_f, 1)
        for i in range(LOW_POOL):
            pool.wait_ge(weights_hi, i + 1)
            nc.gpsimd.tensor_tensor(w_all[1][:, place_of(i)], raw[i % 4][:], w_all[0][:, place_of(i)].bitcast(F32),
                                    ALU.subtract).then_inc(parted, 1)
        pool.wait_ge(place_ready, 1)
        pool.wait_ge(consts_f, 6)
        for k in range(2):
            if k == 1:
                pool.wait_ge(x1_copied, NT)
            for t in range(NT):
                nc.gpsimd.indirect_dma_start(rows_in, bass.IndirectOffsetOnAxis(ap=place[:, k, t:t + 1], axis=0),
                                             xa[k][:, t], None).then_inc(scattered, 16)
        pool.wait_ge(targets_in, 16)
        for j in range(NTILE):
            pool.wait_ge(rows_ready, j + 1)
            nc.gpsimd.indirect_dma_start(rows_out, bass.IndirectOffsetOnAxis(ap=targets[:, j:j + 1], axis=0),
                                         out_rows[j % 4][:], None).then_inc(rows_out_done[j % 4], 16)
        for t in range(NT):
            pool.wait_ge(first_scaled, t + 1)
            nc.gpsimd.tensor_tensor(y[:, t], y_rows[0][:, t], y[:, t], ALU.add).then_inc(first_added, 1)

    @block.scalar
    def _(act):
        def high(i):
            act.wait_ge(w_in[i % 4], 48 * (i // 4 + 1))
            nc.scalar.activation(w_all[0][:, place_of(i)], raw[i % 4][:], ACT.Copy).then_inc(weights_hi, 1)

        def roots(n):
            act.wait_ge(var_ready, n + 1)
            h = slice(n % 2 * GT, (n % 2 + 1) * GT)
            nc.scalar.activation(small[:, 1, h], small[:, 0, h], ACT.Sqrt).then_inc(dev_ready, 1)

        def turned_high(n):
            w, c = n // MC, n % MC
            act.wait_ge(x1_turned, n + 1)
            nc.scalar.activation(xT[0][:, c, w * W:(w + 1) * W], Y_ps[c][w][:], ACT.Copy).then_inc(x1T_hi, 1)

        def silu_of(u):
            act.wait_ge(up_full, u + 1)
            need(act, hid_lo, u - 1)
            nc.scalar.activation(silu[u % 2][:], U_ps[u % 2][:], ACT.Silu).then_inc(silu_ready, 1)

        def hidden_of(u):
            act.wait_ge(gated_ready, u + 1)
            need(act, down_full, u - 1)
            nc.scalar.activation(hidden[0][u % 2][:], silu[u % 2][:], ACT.Copy).then_inc(hid_hi, 1)

        roots(0)
        high(0)
        high(1)
        turned_high(0)
        turned_high(1)
        roots(1)
        high(2)
        high(3)
        turned_high(2)
        turned_high(3)
        for w in range(NW):
            act.wait_ge(flat_full, w + 1)
            nc.scalar.activation(flat_logits[w], flat_ps[w][0:E, :], ACT.Copy).then_inc(flat_copied, 1)
        for i in range(4, 8):
            high(i)
        silu_of(0)
        silu_of(1)
        for i in range(8, LOW_POOL):
            high(i)
        for t in range(NT):
            act.wait_ge(x1_ready, t + 1)
            nc.scalar.activation(xa[1][:, t, 0:M], xa[0][:, t, 0:M], ACT.Copy).then_inc(x1_copied, 1)
        hidden_of(0)
        hidden_of(1)
        for i in range(LOW_POOL, 14):
            high(i)
        silu_of(2)
        silu_of(3)
        hidden_of(2)
        hidden_of(3)
        for i in range(14, NE):
            high(i)
        act.wait_ge(down_full, NS * NW)
        for w in range(NW):
            for m in range(MC):
                nc.scalar.activation(yT[:, m, w * W:(w + 1) * W], Y_ps[m][w][:], ACT.Copy).then_inc(y_copied, 1)

        def step(it, n):
            j = 8 * it + n
            at = j if isinstance(j, int) else NTILE // 2
            if at < NTILE:
                act.wait_ge(tx_full, j + 1)
                need(act, ug_full, j - 1)
                nc.scalar.activation(xtT[0][n % 2][:], TX[n % 2][:, 0:M], ACT.Copy).then_inc(tx_hi, 1)
            if 1 <= at <= NTILE:
                act.wait_ge(ug_full, j)
                need(act, prod_ready, j - 2)
                need(act, ht_full, j - 2)
                nc.scalar.activation(act_t[(n - 1) % 2][:], UG[(n - 1) % 2][:, 0:F], ACT.Silu
                                     ).then_inc(act_ready, 1)
            if 2 <= at <= NTILE + 1:
                act.wait_ge(ht_full, j - 1)
                need(act, dn_full, j - 3)
                nc.scalar.activation(hT[0][n % 2][:], HT[n % 2][:, 0:P], ACT.Copy).then_inc(ht_hi, 1)
            if 3 <= at:
                act.wait_ge(dn_full, j - 2)
                if at >= 7:
                    act.wait_ge(rows_out_done[(n - 3) % 4], 16 * (2 * it + (n - 3) // 4))
                nc.scalar.activation(out_rows[(n - 3) % 4][:], DN[(n - 3) % 2][:, 0:M], ACT.Copy
                                     ).then_inc(rows_ready, 1)

        act.wait_ge(sum_ready, NT // 2)
        tile_walk(act, step)
        act.wait_ge(shifted, 1)
        nc.scalar.activation(score[:], score[:], ACT.Exp).then_inc(exp_ready, 1)

        def scale_first(t):
            act.wait_ge(y_in[0][t], 16)
            nc.scalar.activation(y_rows[0][:, t], y_rows[0][:, t], ACT.Copy, scale=share[:, 0, t:t + 1]
                                 ).then_inc(first_scaled, 1)

        act.wait_ge(share_ready, 1)
        for t in range(6):
            scale_first(t)
        for h in range(2):
            roots(2 + h)
            if h == 0:
                scale_first(6)
                scale_first(7)
            for t in range(h * GT, min((h + 1) * GT, NT - 2)):
                act.wait_ge(norm_ready, h + 1)
                nc.scalar.activation(y[:, t], y[:, t], ACT.Identity, scale=small[:, 6, t:t + 1],
                                     bias=small[:, 7, t:t + 1]).then_inc(y_ready, 1)

    @block.vector
    def _(dve):
        steps = [0]

        def ordered(ins):
            steps[0] += 1
            ins.then_inc(dve_step, 1)
            dve.wait_ge(dve_step, steps[0])

        def variances(h):
            for t in range(h * GT, (h + 1) * GT):
                ins = nc.vector.bn_aggr(mean_var[:, t], stats[:, t])
            ordered(ins)
            cols = slice(h * GT, (h + 1) * GT)
            nc.vector.tensor_scalar(small[:, 0, cols], mean_var[:, cols, 1], EPS, None, ALU.add
                                    ).then_inc(var_ready, 1)

        def inverses(h, n):
            cols = slice(h * GT, (h + 1) * GT)
            dve.wait_ge(dev_ready, n + 1)
            ordered(nc.vector.reciprocal(small[:, 2, cols], small[:, 1, cols]))
            ordered(nc.vector.tensor_tensor(small[:, 3, cols], small[:, 2, cols], small[:, 0, cols], ALU.mult))
            ordered(nc.vector.tensor_tensor(small[:, 4, cols], small[:, 3, cols], small[:, 1, cols], ALU.add))
            ordered(nc.vector.tensor_scalar(small[:, 5, cols], small[:, 4, cols], 0.5, None, ALU.mult))
            ordered(nc.vector.reciprocal(small[:, 6, cols], small[:, 5, cols]))

        def turned_low(n):
            w, c = n // MC, n % MC
            cols = slice(w * W, (w + 1) * W)
            dve.wait_ge(x1T_hi, n + 1)
            nc.vector.tensor_tensor(xT[1][:, c, cols], Y_ps[c][w][:], xT[0][:, c, cols].bitcast(F32),
                                    ALU.subtract).then_inc(x1T_lo, 1)

        x1 = xa[0]
        for h in range(2):
            for b in range(2 * h, 2 * h + 2):
                dve.wait_ge(r_turned, b + 1)
                both = slice(2 * b, 2 * b + 2)
                ordered(nc.vector.tensor_tensor(x1[:, both, 0:M], banks[b][:].rearrange("p (t m) -> p t m", m=M),
                                                x1[:, both, 0:M], ALU.add))
                for t in range(2 * b, 2 * b + 2):
                    ins = nc.vector.bn_stats(stats[:, t], x1[:, t, 0:M])
                ordered(ins)
            variances(h)
            if h == 0:
                dve.wait_ge(rw_turned, 1)
                turned = rw_ps[:, 0:MC * E].rearrange("p (c e) -> p c e", c=MC)
                ordered(nc.vector.tensor_copy(rwT[0][:], turned))
                nc.vector.tensor_tensor(rwT[1][:], turned, rwT[0][:].bitcast(F32), ALU.subtract).then_inc(rw_ready, 1)
            else:
                turned_low(0)
                turned_low(1)
            inverses(h, h)
            for t in range(h * GT, (h + 1) * GT):
                nc.vector.tensor_scalar(x1[:, t, 0:M], x1[:, t, 0:M], mean_var[:, t, 0:1], small[:, 6, t:t + 1],
                                        ALU.subtract, ALU.mult).then_inc(x1_ready, 1)
        turned_low(2)
        turned_low(3)
        per_token = lambda a: a.unsqueeze(2).to_broadcast([P, NT, E])
        per_expert = lambda a: a.unsqueeze(1).to_broadcast([P, NT, E])
        dve.wait_ge(logits_full, 1)
        dve.wait_ge(router_in, 32)
        dve.wait_ge(consts_f, 6)
        got = logits_ps[:, 0:NT * E].rearrange("p (t e) -> p t e", t=NT)
        nc.vector.tensor_copy(iota[:], iota_i[:])
        nc.vector.tensor_copy(tile_f[:], tile_i[:])
        ordered(nc.vector.tensor_tensor(biased[:], got, per_expert(bias[:]), ALU.add))
        nc.vector.tensor_copy(logits[:], got)
        for t in range(NT):
            ins = nc.vector.max(top[:, t], biased[:, t])
        ordered(ins)
        nc.vector.tensor_reduce(small[:, 0], logits[:], AX.X, ALU.max)
        for t in range(NT):
            ins = nc.vector.max_index(top_i[:, t], top[:, t], biased[:, t])
        ordered(ins)
        nc.vector.tensor_tensor(score[:], logits[:], per_token(small[:, 0]), ALU.subtract).then_inc(shifted, 1)
        ordered(nc.vector.tensor_copy(top_f[:], top_i[:]))
        for k in range(2):
            ins = nc.vector.tensor_tensor(chosen[:, k], per_expert(iota[:]), per_token(top_f[:, :, k]),
                                          ALU.is_equal)
        ordered(ins)
        nc.vector.tensor_tensor(chosen_b[:, 0:NT], chosen[:, 0], chosen[:, 1], ALU.add).then_inc(chosen_ready, 1)
        dve.wait_ge(ranks_full, 1)
        ranks = rank_ps[:, 0:(NT + 1) * E].rearrange("p (t e) -> p t e", e=E)
        ordered(nc.vector.tensor_scalar(small[:, 0], iota[:, 0:NT], float(P), None, ALU.mult))
        ordered(nc.vector.tensor_tensor(wide[:, :, 0:NT], ranks[:, NT].unsqueeze(2).to_broadcast([P, E, NT]),
                                        small[:, 0].unsqueeze(1).to_broadcast([P, E, NT]), ALU.is_gt))
        ordered(nc.vector.tensor_reduce(tiles[:], wide[:, :, 0:NT], AX.X, ALU.add))
        ordered(nc.vector.tensor_tensor(wide[:], upto[:], tiles[:].unsqueeze(1).to_broadcast([P, E, E]), ALU.mult))
        ordered(nc.vector.tensor_reduce(ends[:], wide[:], AX.X, ALU.add))
        ordered(nc.vector.tensor_tensor(tiles[:], ends[:], tiles[:], ALU.subtract))
        ordered(nc.vector.tensor_scalar(tiles[:], tiles[:], float(P), None, ALU.mult))
        ordered(nc.vector.tensor_tensor(biased[:], ranks[:, 0:NT], per_expert(tiles[:]), ALU.add))
        for k in range(2):
            ins = nc.vector.tensor_tensor(picked[:, k], chosen[:, k], biased[:], ALU.mult)
        ordered(ins)
        ordered(nc.vector.tensor_reduce(place_f[:], picked[:], AX.X, ALU.add))
        nc.vector.tensor_copy(place[:], place_f[:]).then_inc(place_ready, 1)

        def gate(u):
            dve.wait_ge(silu_ready, u + 1)
            dve.wait_ge(gate_full, u + 1)
            nc.vector.tensor_tensor(silu[u % 2][:], G_ps[u % 2][:], silu[u % 2][:], ALU.mult
                                    ).then_inc(gated_ready, 1)

        def hidden_low(u):
            dve.wait_ge(hid_hi, u + 1)
            nc.vector.tensor_tensor(hidden[1][u % 2][:], silu[u % 2][:], hidden[0][u % 2][:].bitcast(F32),
                                    ALU.subtract).then_inc(hid_lo, 1)

        def low(i):
            dve.wait_ge(weights_hi, i + 1)
            nc.vector.tensor_tensor(w_all[1][:, place_of(i)], raw[i % 4][:], w_all[0][:, place_of(i)].bitcast(F32),
                                    ALU.subtract).then_inc(parted_dve, 1)

        gate(0)
        gate(1)
        hidden_low(0)
        hidden_low(1)
        for i in range(LOW_POOL, 14):
            low(i)
        ordered(nc.vector.tensor_tensor(owner_w[:], ends[0:1].unsqueeze(1).to_broadcast([1, NPACK, E]),
                                        tile_f[:].unsqueeze(2).to_broadcast([1, NPACK, E]), ALU.is_le))
        ordered(nc.vector.tensor_reduce(owner_f[:], owner_w[:], AX.X, ALU.add))
        ordered(nc.vector.tensor_scalar(owner_f[:], owner_f[:], float(E - 1), None, ALU.min))
        by_word = owner_f[:].rearrange("o (i k) -> o i k", k=4)
        at = lambda k: by_word[:, k // 4:k // 4 + NWORD, k % 4]
        ordered(nc.vector.tensor_copy(packed_f[:], at(0)))
        for k in range(1, 6):
            ordered(nc.vector.scalar_tensor_tensor(packed_f[:], at(k), float(16 ** k), packed_f[:],
                                                   ALU.mult, ALU.add))
        nc.vector.tensor_copy(packed[:], packed_f[:]).then_inc(owner_ready, 1)
        gate(2)
        gate(3)
        hidden_low(2)
        hidden_low(3)
        for i in range(14, NE):
            low(i)
        for b in range(NT // 2):
            dve.wait_ge(y_turned, b + 1)
            both = slice(2 * b, 2 * b + 2)
            nc.vector.tensor_tensor(y[:, both], banks[b][:].rearrange("p (t m) -> p t m", m=M),
                                    x1[:, both, 0:M], ALU.add).then_inc(sum_ready, 1)

        def step(it, n):
            j = 8 * it + n
            at = j if isinstance(j, int) else NTILE // 2
            if at < NTILE:
                dve.wait_ge(tx_hi, j + 1)
                nc.vector.tensor_tensor(xtT[1][n % 2][:], TX[n % 2][:, 0:M], xtT[0][n % 2][:].bitcast(F32),
                                        ALU.subtract).then_inc(tx_lo, 1)
            if 1 <= at <= NTILE:
                dve.wait_ge(act_ready, j)
                slot = act_t[(n - 1) % 2]
                nc.vector.tensor_tensor(slot[:], UG[(n - 1) % 2][:, F:2 * F], slot[:], ALU.mult
                                        ).then_inc(prod_ready, 1)
            if 2 <= at <= NTILE + 1:
                dve.wait_ge(ht_hi, j - 1)
                nc.vector.tensor_tensor(hT[1][n % 2][:], HT[n % 2][:, 0:P], hT[0][n % 2][:].bitcast(F32),
                                        ALU.subtract).then_inc(ht_lo, 1)

        tile_walk(dve, step)
        dve.wait_ge(exp_ready, 1)
        ordered(nc.vector.tensor_reduce(small[:, 1], score[:], AX.X, ALU.add))
        ordered(nc.vector.reciprocal(small[:, 2], small[:, 1]))
        ordered(nc.vector.tensor_tensor(score[:], score[:], per_token(small[:, 2]), ALU.mult))
        for k in range(2):
            ins = nc.vector.tensor_tensor(picked[:, k], chosen[:, k], score[:], ALU.mult)
        ordered(ins)
        ordered(nc.vector.tensor_reduce(share[:], picked[:], AX.X, ALU.add))
        ordered(nc.vector.tensor_tensor(small[:, 3], share[:, 0], share[:, 1], ALU.add))
        ordered(nc.vector.reciprocal(small[:, 4], small[:, 3]))
        nc.vector.tensor_tensor(share[:], share[:], small[:, 4].unsqueeze(1).to_broadcast([P, 2, NT]),
                                ALU.mult).then_inc(share_ready, 1)
        dve.wait_ge(share_ready, 1)
        dve.wait_ge(sum_ready, NT // 2)
        for h in range(2):
            for t in range(h * GT, (h + 1) * GT):
                dve.wait_ge(y_in[1][t], 16)
                dve.wait_ge(first_added, t + 1)
                ordered(nc.vector.scalar_tensor_tensor(y[:, t], y_rows[1][:, t], share[:, 1, t:t + 1],
                                                       y[:, t], ALU.mult, ALU.add))
                ins = nc.vector.bn_stats(stats[:, t], y[:, t])
            ordered(ins)
            variances(h)
            inverses(h, 2 + h)
            cols = slice(h * GT, (h + 1) * GT)
            ordered(nc.vector.tensor_tensor(small[:, 5, cols], mean_var[:, cols, 0], small[:, 6, cols], ALU.mult))
            nc.vector.tensor_scalar(small[:, 7, cols], small[:, 5, cols], -1.0, None, ALU.mult
                                    ).then_inc(norm_ready, 1)
        for t in range(NT - 2, NT):
            nc.vector.tensor_scalar(y[:, t], y[:, t], mean_var[:, t, 0:1], small[:, 6, t:t + 1],
                                    ALU.subtract, ALU.mult).then_inc(tail_ready, 1)

    @block.tensor
    def _(pe):
        pe.wait_ge(ident_ready, 1)

        def turn_back(src, turned, copied):
            for b in range(NT // 2):
                if copied:
                    pe.wait_ge(y_copied, MC * (b // 2 + 1))
                for t in range(2 * b, 2 * b + 2):
                    for c in range(MC):
                        ins = pe.transpose(banks[b][:, (t % 2) * M + c * P:(t % 2) * M + (c + 1) * P],
                                           src[:, c, t * P:(t + 1) * P], ident[:])
                ins.then_inc(turned, 1)

        def flat_logits_of(w):
            pe.wait_ge(x1T_lo, MC * (w + 1))
            pe.wait_ge(rw_ready, 1)
            for c in range(MC):
                ins = three(pe, flat_ps[w][0:E, :], [rwT[a][:, c] for a in range(2)],
                            [xT[a][:, c, w * W:(w + 1) * W] for a in range(2)], c == 0, c == MC - 1)
            ins.then_inc(flat_full, 1)

        turn_back(r_acc, r_turned, False)
        pe.wait_ge(router_in, 32)
        for c in range(MC):
            ins = pe.transpose(rw_ps[:, c * E:(c + 1) * E], rw[:, c * P:(c + 1) * P], ident[0:E, 0:E])
        ins.then_inc(rw_turned, 1)
        for w in range(NW):
            pe.wait_ge(x1_ready, GT * (w + 1))
            if w == 1:
                pe.wait_ge(rw_ready, 1)
            for c in range(MC):
                for a in range(GT):
                    ins = pe.transpose(Y_ps[c][w][:, a * P:(a + 1) * P],
                                       xa[0][:, w * GT + a, c * P:(c + 1) * P], ident[:])
                ins.then_inc(x1_turned, 1)
            if w == 1:
                flat_logits_of(0)
        flat_logits_of(1)
        for t in range(NT):
            pe.wait_ge(flat_copied, t // GT + 1)
            ins = pe.transpose(logits_ps[:, t * E:(t + 1) * E], flat_logits[t // GT][:, t % GT * P:(t % GT + 1) * P], ident[0:E, 0:E])
        ins.then_inc(logits_full, 1)

        def up_gate(u):
            i, w = u // NW, u % NW
            pe.wait_ge(parted, i + 1)
            need(pe, gated_ready, u - 1)
            for g, bank, full in ((0, U_ps[u % 2], up_full), (1, G_ps[u % 2], gate_full)):
                for c in range(MC):
                    cols = slice((c * 2 + g) * F, (c * 2 + g + 1) * F)
                    ins = three(pe, bank[:], [w_all[a][:, E + i, cols] for a in range(2)],
                                [xT[a][:, c, w * W:(w + 1) * W] for a in range(2)], c == 0, c == MC - 1)
                ins.then_inc(full, 1)

        def down(u):
            i, w = u // NW, u % NW
            pe.wait_ge(hid_lo, u + 1)
            for m in range(MC):
                cols = slice(2 * MC * F + m * P, 2 * MC * F + (m + 1) * P)
                ins = three(pe, Y_ps[m][w][:], [w_all[a][:, E + i, cols] for a in range(2)],
                            [hidden[a][u % 2][:] for a in range(2)], i == 0, i == NS - 1)
            ins.then_inc(down_full, 1)

        up_gate(0)
        pe.wait_ge(consts_f, 6)
        pe.wait_ge(chosen_ready, 1)
        every = rank_ps[:, 0:(NT + 1) * E]
        pe.matmul(every, below[:], chosen_b[:].rearrange("p t e -> p (t e)"), start=True, stop=False)
        for t in range(NT):
            ins = pe.matmul(every.rearrange("p (t e) -> p t e", e=E)[:, t + 1:NT + 1], ones[:],
                            chosen_b[:, t:t + 1].to_broadcast([P, NT - t, E]), start=False, stop=t == NT - 1)
        ins.then_inc(ranks_full, 1)
        up_gate(1)
        pe.wait_ge(place_ready, 1)
        down(0)
        up_gate(2)
        down(1)
        up_gate(3)
        down(2)
        down(3)
        turn_back(yT, y_turned, True)

        word = [None]

        def expert_of(n, back):
            k = n % 4 + 3 - back
            return word[0] // 16 ** k % 16

        def step(it, n):
            j = 8 * it + n
            at = j if isinstance(j, int) else NTILE // 2
            if at < NTILE:
                pe.wait_ge(rows_read[n % 4], 16 * (2 * it + n // 4 + 1))
                need(pe, tx_lo, j - 1)
                for c in range(MC):
                    ins = pe.transpose(TX[n % 2][:, c * P:(c + 1) * P], x_rows[n % 4][:, c * P:(c + 1) * P],
                                       ident[:])
                ins.then_inc(tx_full, 1)
            if n % 4 == 0:
                word[0] = pe.value_load(packed[0:1, bass.ds(2 * it + n // 4, 1)], min_val=0,
                                        max_val=16 ** 6 - 1)
            if 1 <= at <= NTILE:
                e = expert_of(n, 1)
                pe.wait_ge(tx_lo, j)
                need(pe, prod_ready, j - 2)
                for c in range(MC):
                    ins = three(pe, UG[(n - 1) % 2][:, 0:2 * F],
                                [xtT[a][(n - 1) % 2][:, c * P:(c + 1) * P] for a in range(2)],
                                [w_all[a][:, bass.ds(e, 1), c * 2 * F:(c + 1) * 2 * F].rearrange(
                                    "p o f -> p (o f)") for a in range(2)], c == 0, c == MC - 1)
                ins.then_inc(ug_full, 1)
            if 2 <= at <= NTILE + 1:
                pe.wait_ge(prod_ready, j - 1)
                need(pe, ht_lo, j - 3)
                pe.transpose(HT[n % 2][:, 0:P], act_t[n % 2][:], ident[:]).then_inc(ht_full, 1)
            if 3 <= at:
                e = expert_of(n, 3)
                pe.wait_ge(ht_lo, j - 2)
                three(pe, DN[(n - 3) % 2][:, 0:M], [hT[a][(n - 3) % 2][:] for a in range(2)],
                      [w_all[a][:, bass.ds(e, 1), 2 * MC * F:RAW].rearrange("p o f -> p (o f)")
                       for a in range(2)], True, True).then_inc(dn_full, 1)

        pe.wait_ge(sum_ready, NT // 2)
        pe.wait_ge(parted, LOW_POOL)
        pe.wait_ge(parted_dve, NE - LOW_POOL)
        pe.wait_ge(owner_ready, 1)
        tile_walk(pe, step, 4)


_INS = ['L0_attn_x', 'L0_attn_w_aq', 'L0_attn_w_ak', 'L0_attn_w_av', 'L0_attn_w_ao', 'L0_ffn_router_w',
        'L0_ffn_router_bias', 'L0_ffn_Wu', 'L0_ffn_Wg', 'L0_ffn_Wd', 'L0_ffn_Su', 'L0_ffn_Sg', 'L0_ffn_Sd']


def layer(nc, x, wq, wk, wv, wo, router_w, router_b, wu, wg, wd, su, sg, sd, cos_t, sin_t, out):
    rows_in = nc.dram_tensor("rows_in", (NTILE * P, M + 1), F32, kind="Internal").ap()
    rows_out = nc.dram_tensor("rows_out", ((2 * NT + NTILE) * P, M), F32, kind="Internal").ap()
    with (nc.sbuf_tensor("r_acc", [P, MC, T], F32) as r_acc,
          nc.sbuf_tensor("x_place", [P, NT * (M + 1)], F32) as x_place):
        with ExitStack() as ctx:
            attention(nc, ctx, x, wq, wk, wv, wo, cos_t, sin_t, rows_in, x_place, r_acc)
        with ExitStack() as ctx:
            xa = [x_place[:].rearrange("p (t m) -> p t m", t=NT),
                  ctx.enter_context(nc.sbuf_tensor("xa1", [P, NT, M + 1], F32))]
            y = r_acc[:].rearrange("p c t -> p (c t)").rearrange("p (t m) -> p t m", m=M)
            experts(nc, ctx, router_w, router_b, wu, wg, wd, su, sg, sd, rows_in, rows_out, xa, y, r_acc,
                    out)


def rotary_tables():
    freqs = np.power(float(ROTARY_BASE), -np.arange(D // 2) / (D // 2)).astype(np.float32)
    angles = (np.arange(T, dtype=np.float32)[None, :] * freqs[:, None]).astype(np.float32)
    cos, sin = np.cos(angles.astype(np.float64)), np.sin(angles.astype(np.float64))
    return (np.concatenate([cos, cos]).astype(np.float32), np.concatenate([-sin, sin]).astype(np.float32))


def kernel(**inputs):
    import concourse.bacc as _bacc
    from concourse.bass_utils import run_bass_kernel_spmd as _run

    nc = _bacc.Bacc("TRN2", target_bir_lowering=False, num_devices=1)
    arrays, args = {}, []
    for name in _INS:
        arrays[name] = np.ascontiguousarray(inputs[name])
    arrays["cos_t"], arrays["sin_t"] = rotary_tables()
    for name, a in arrays.items():
        args.append(nc.dram_tensor(name, a.shape, mybir.dt.from_np(a.dtype), kind="ExternalInput").ap())
    args.append(nc.dram_tensor("out", (1, T, M), F32, kind="ExternalOutput").ap())
    layer(nc, *args)
    return _run(nc, [arrays], core_ids=[0]).results[0]["out"]
```
